# Optimizing a Trainium2 kernel written in Bass

```python
import numpy as np
import jax
import jax.numpy as jnp

def _softmax(x, axis=-1):
    return jax.nn.softmax(x, axis=axis)

def _gelu(x):
    return jax.nn.gelu(x, approximate=True)

def _silu(x):
    return jax.nn.silu(x)

def _sigmoid(x):
    return jax.nn.sigmoid(x)

def _layernorm(x, axis=-1, eps=1e-05):
    m = jnp.mean(x, axis=axis, keepdims=True)
    v = jnp.var(x, axis=axis, keepdims=True)
    return (x - m) / jnp.sqrt(v + eps)

def _scatter_add(tgt, idx, src, axis=0):
    return tgt.at[idx].add(src)

def _segment_sum(src, seg, n):
    return jax.ops.segment_sum(src, seg, n)
kernel_name = 'mk_metaformer_d1_conv_nhwc512_r4_15d77f'

def setup_inputs(seed: int=0):
    np.random.seed(seed)
    _w = jnp.asarray

    def _rec_inputs():
        import jax
        import jax.numpy as jnp
        _gk = jax.random.key(seed)
        x = -0.000125 + 0.9999 * jax.random.normal(jax.random.fold_in(_gk, 1), (16, 16, 16, 128), jnp.float32)
        return x
    x = _rec_inputs()

    def _L0_conv_setup():
        import jax, jax.numpy as jnp
        import numpy as np
        GROUPS = 8
        STRIDES = (1, 1)
        DILATION = (1, 1)
        key = jax.random.key(seed)
        k1, k2, k3 = jax.random.split(key, 3)
        inputs = jax.random.normal(k1, (16, 16, 16, 128), dtype=jnp.float32)
        kernel = jax.random.normal(k2, (3, 3, 128 // GROUPS, 128), dtype=jnp.float32) * 0.05
        bias = jax.random.normal(k3, (128,), dtype=jnp.float32) * 0.05
        return {'inputs': inputs, 'kernel': kernel, 'bias': bias}
    _L0_conv_all = _L0_conv_setup()
    _L0_conv_in = {k: v for k, v in _L0_conv_all.items() if k in ('kernel', 'bias')}
    del _L0_conv_all

    def _L0_ffn_setup():
        import jax, jax.numpy as jnp
        import numpy as np
        B, S, D, H, E, K = (2, 512, 128, 256, 8, 2)

        def _moe(x, router_w, w_gate, w_up, w_down):
            bsz, seq, d = x.shape
            flat = x.reshape(-1, d)
            logits = flat @ router_w.T
            topk_vals, topk_idx = jax.lax.top_k(logits, K)
            topk_w = jax.nn.softmax(topk_vals, axis=-1)
            s = flat.shape[0]
            dense_w = jnp.zeros((s, E), dtype=flat.dtype).at[jnp.arange(s)[:, None], topk_idx].add(topk_w)
            g = jnp.einsum('sd,edh->esh', flat, w_gate)
            u = jnp.einsum('sd,edh->esh', flat, w_up)
            y = jnp.einsum('esh,ehd->esd', jax.nn.silu(g) * u, w_down)
            out = jnp.einsum('esd,se->sd', y, dense_w)
            return out.reshape(bsz, seq, d)
        key = jax.random.key(seed)
        k1, k2, k3, k4, k5 = jax.random.split(key, 5)
        return {'x': jax.random.normal(k1, (B, S, D), dtype=jnp.float32), 'router_w': jax.random.normal(k2, (E, D), dtype=jnp.float32) * D ** (-0.5), 'w_gate': jax.random.normal(k3, (E, D, H), dtype=jnp.float32) * D ** (-0.5), 'w_up': jax.random.normal(k4, (E, D, H), dtype=jnp.float32) * D ** (-0.5), 'w_down': jax.random.normal(k5, (E, H, D), dtype=jnp.float32) * H ** (-0.5)}
    _L0_ffn_all = _L0_ffn_setup()
    _L0_ffn_in = {k: v for k, v in _L0_ffn_all.items() if k in ('router_w', 'w_gate', 'w_up', 'w_down')}
    del _L0_ffn_all
    return {'x': x, 'L0_conv_kernel': _L0_conv_in['kernel'], 'L0_conv_bias': _L0_conv_in['bias'], 'L0_ffn_router_w': _L0_ffn_in['router_w'], 'L0_ffn_w_gate': _L0_ffn_in['w_gate'], 'L0_ffn_w_up': _L0_ffn_in['w_up'], 'L0_ffn_w_down': _L0_ffn_in['w_down']}

def reference(x, L0_conv_kernel, L0_conv_bias, L0_ffn_router_w, L0_ffn_w_gate, L0_ffn_w_up, L0_ffn_w_down):
    import jax
    import jax.numpy as jnp

    def _L0_conv_ref(inputs, kernel, bias):
        import jax, jax.numpy as jnp
        import numpy as np
        GROUPS = 8
        STRIDES = (1, 1)
        DILATION = (1, 1)
        out = jax.lax.conv_general_dilated(inputs, kernel, window_strides=STRIDES, padding='SAME', rhs_dilation=DILATION, dimension_numbers=('NHWC', 'HWIO', 'NHWC'), feature_group_count=GROUPS)
        out = out + bias
        return jax.nn.relu(out)

    def _L0_ffn_ref(x, router_w, w_gate, w_up, w_down):
        import jax, jax.numpy as jnp
        import numpy as np
        B, S, D, H, E, K = (2, 512, 128, 256, 8, 2)

        def _moe(x, router_w, w_gate, w_up, w_down):
            bsz, seq, d = x.shape
            flat = x.reshape(-1, d)
            logits = flat @ router_w.T
            topk_vals, topk_idx = jax.lax.top_k(logits, K)
            topk_w = jax.nn.softmax(topk_vals, axis=-1)
            s = flat.shape[0]
            dense_w = jnp.zeros((s, E), dtype=flat.dtype).at[jnp.arange(s)[:, None], topk_idx].add(topk_w)
            g = jnp.einsum('sd,edh->esh', flat, w_gate)
            u = jnp.einsum('sd,edh->esh', flat, w_up)
            y = jnp.einsum('esh,ehd->esd', jax.nn.silu(g) * u, w_down)
            out = jnp.einsum('esd,se->sd', y, dense_w)
            return out.reshape(bsz, seq, d)
        return _moe(x, router_w, w_gate, w_up, w_down)

    def _gn(v, G=32, eps=1e-05):
        B_, H_, W_, C_ = v.shape
        g = v.reshape(B_, H_, W_, G, C_ // G)
        m = jnp.mean(g, axis=(1, 2, 4), keepdims=True)
        s = jnp.var(g, axis=(1, 2, 4), keepdims=True)
        return ((g - m) / jnp.sqrt(s + eps)).reshape(v.shape)

    def _ln_c(v, eps=1e-06):
        m = jnp.mean(v, axis=-1, keepdims=True)
        s = jnp.var(v, axis=-1, keepdims=True)
        return (v - m) / jnp.sqrt(s + eps)

    def _ln_t(v, eps=1e-05):
        m = jnp.mean(v, axis=-1, keepdims=True)
        s = jnp.var(v, axis=-1, keepdims=True)
        return (v - m) / jnp.sqrt(s + eps)

    def _to_tokens(v):
        B_, H_, W_, C_ = v.shape
        return v.reshape(B_, H_ * W_, C_)

    def _from_tokens(t, like):
        return t.reshape(like.shape)
    x = x + _L0_conv_ref(_ln_c(x), L0_conv_kernel, L0_conv_bias)
    t = _to_tokens(x)
    t = t + _L0_ffn_ref(_ln_t(t), L0_ffn_router_w, L0_ffn_w_gate, L0_ffn_w_up, L0_ffn_w_down)
    x = _from_tokens(t, x)
    return x

_drawn_inputs = setup_inputs


def setup_inputs(seed=0):
    import zlib

    import numpy as np

    out = dict(_drawn_inputs(seed))
    spreads = {}
    factors = {}
    for name, (base, spread) in spreads.items():
        noise = np.random.default_rng([zlib.crc32(name.encode()), seed]).standard_normal(out[name].shape)
        drawn = base * np.exp(spread * noise) if base else spread * noise
        out[name] = jnp.asarray(drawn.astype(out[name].dtype))
    for name, factor in factors.items():
        out[name] = (out[name] * factor).astype(out[name].dtype)
    return out
```

```python
from contextlib import ExitStack

import numpy as np

import concourse.bass as bass
from concourse import mybir

ALU = mybir.AluOpType
ACT = mybir.ActivationFunctionType
F32 = mybir.dt.float32
F32R = mybir.dt.float32r
U32 = mybir.dt.uint32

P = 128
IMG, HH, WW = 2, 16, 16
N = IMG * HH * WW
TT = N // P
E = 8
J = 2
TAPS = 9
GROUPS = 8
GC = P // GROUPS
EPS_CONV, EPS_FFN = 1e-6, 1e-5
WBQ = 4


def metaformer_moe(nc, x, conv_k, conv_b, router_t, expert_w, out):
    chunks = x.shape[0] // IMG
    x_tok = x.rearrange("b h w c -> (b h w) c").rearrange("(n t p) c -> n p t c", t=TT, p=P)
    out_tok = out.rearrange("b h w c -> (b h w) c").rearrange("(n t p) c -> n p t c", t=TT, p=P)
    wb_dram = nc.dram_tensor("wb_dram", [chunks, E * N], F32, kind="Internal").ap()

    with ExitStack() as ctx:
        def sb(name, shape, dt=F32):
            return ctx.enter_context(nc.sbuf_tensor(name, shape, dt))

        def sem(name):
            return ctx.enter_context(nc.semaphore(name))

        ident = sb("ident", [P, P])
        iota8 = sb("iota8", [P, E])
        neghalf = sb("neghalf", [P, TT])
        bias = sb("bias", [P, 1])
        ck = sb("ck", [P, TAPS, P])
        ck_hi, ck_lo = sb("ck_hi", [P, TAPS, P], F32R), sb("ck_lo", [P, TAPS, P], F32R)
        rw = sb("rw", [P, E])
        rw_hi, rw_lo = sb("rw_hi", [P, E], F32R), sb("rw_lo", [P, E], F32R)
        ew = sb("ew", [P, E, 3 * J, P])
        ew_hi, ew_lo = sb("ew_hi", [P, E, 3 * J, P], F32R), sb("ew_lo", [P, E, 3 * J, P], F32R)
        xt = [sb(f"xt{b}", [P, TT, P]) for b in range(2)]
        xn = sb("xn", [P, TT, P])
        pad_hi = sb("pad_hi", [P, IMG, HH + 2, WW + 2], F32R)
        pad_lo = sb("pad_lo", [P, IMG, HH + 2, WW + 2], F32R)
        relu = sb("relu", [P, N])
        tt = [sb(f"tt{b}", [P, TT, P]) for b in range(2)]
        zn = sb("zn", [P, TT, P])
        z_hi = [sb(f"z_hi{b}", [P, N], F32R) for b in range(2)]
        z_lo = [sb(f"z_lo{b}", [P, N], F32R) for b in range(2)]
        bn1, bn2 = sb("bn1", [P, TT, 6]), sb("bn2", [P, TT, 6])
        mv1, mv2 = sb("mv1", [P, TT, 2]), sb("mv2", [P, TT, 2])
        ln1, ln2 = sb("ln1", [P, 4, TT]), sb("ln2", [P, 4, TT])
        logits = sb("logits", [P, TT, E])
        top = sb("top", [P, TT, E])
        topi = sb("topi", [P, TT, E], U32)
        gap = sb("gap", [P, TT])
        th = sb("th", [P, TT])
        w12 = sb("w12", [P, 2, TT])
        hot = sb("hot", [P, 2, E, TT])
        dense = sb("dense", [P, P])
        denseT = sb("denseT", [E * TT, P])
        wb = [sb(f"wb{b}", [P, E, N]) for b in range(2)]
        sg = sb("sg", [P, 2, J, N])
        hh = sb("hh", [P, 2, J, N])
        h_hi, h_lo = sb("h_hi", [P, 2, J, N], F32R), sb("h_lo", [P, 2, J, N], F32R)
        yw = sb("yw", [P, 2, N])
        acc = [sb(f"acc{b}", [P, N]) for b in range(2)]
        res = sb("res", [P, TT, P])

        ps_g = [ctx.enter_context(nc.psum_tensor(f"ps_g{j}", [P, N], F32)) for j in range(J)]
        ps_u = [ctx.enter_context(nc.psum_tensor(f"ps_u{j}", [P, N], F32)) for j in range(J)]
        ps_y = [ctx.enter_context(nc.psum_tensor(f"ps_y{b}", [P, N], F32)) for b in range(2)]
        ps_a = ctx.enter_context(nc.psum_tensor("ps_a", [P, N], F32))
        ps_b = ctx.enter_context(nc.psum_tensor("ps_b", [P, N], F32))

        x_loaded = [sem(f"x_loaded{b}") for b in range(2)]
        ck_loaded, bias_loaded, rw_loaded = sem("ck_loaded"), sem("bias_loaded"), sem("rw_loaded")
        ew_loaded = [sem(f"ew_loaded{q}") for q in range(E)]
        wb_out, out_stored = sem("wb_out"), sem("out_stored")
        wb_loaded = [sem(f"wb_loaded{q}") for q in range(WBQ)]
        ck_zeroed, ident_zeroed, ident_ready, consts_ready = (
            sem("ck_zeroed"), sem("ident_zeroed"), sem("ident_ready"), sem("consts_ready"))
        neghalf_ready, iota_ready = sem("neghalf_ready"), sem("iota_ready")
        ck_hi_ready, ck_lo_ready = sem("ck_hi_ready"), sem("ck_lo_ready")
        rw_hi_ready, rw_lo_ready = sem("rw_hi_ready"), sem("rw_lo_ready")
        ew_hi_ready, ew_lo_ready = sem("ew_hi_ready"), sem("ew_lo_ready")
        mv1_ready, xn_ready, xnT_ready = sem("mv1_ready"), sem("xn_ready"), sem("xnT_ready")
        pad_hi_ready, pad_lo_ready, conv_ready = sem("pad_hi_ready"), sem("pad_lo_ready"), sem("conv_ready")
        relu_ready, reluT_ready, t_ready = sem("relu_ready"), sem("reluT_ready"), sem("t_ready")
        mv2_ready, zn_ready, znT_ready = sem("mv2_ready"), sem("zn_ready"), sem("znT_ready")
        z_hi_ready, z_lo_ready, logits_ready = sem("z_hi_ready"), sem("z_lo_ready"), sem("logits_ready")
        gap_ready, th_ready, dense_ready = sem("gap_ready"), sem("th_ready"), sem("dense_ready")
        denseT_ps_ready, denseT_ready = sem("denseT_ps_ready"), sem("denseT_ready")
        passed = sem("passed")
        dve_step, pool_step = sem("dve_step"), sem("pool_step")
        g_ready, u_ready, sg_ready, h_ready = sem("g_ready"), sem("u_ready"), sem("sg_ready"), sem("h_ready")
        h_hi_ready, h_lo_ready, y_ready = sem("h_hi_ready"), sem("h_lo_ready"), sem("y_ready")
        yw_ready, acc_ready, accT_ready, res_ready = sem("yw_ready"), sem("acc_ready"), sem("accT_ready"), sem("res_ready")

        img = "p (b h w) -> p b h w"
        tile4 = "p (t c) -> p t c"
        LINKS_LN = 3

        block = ctx.enter_context(nc.Block())

        @block.sync
        def _(sp):
            def load_x(n, b):
                sp.dma_start(xt[b][:], x_tok[bass.ds(n, 1)].rearrange("a p t c -> p (a t) c")
                             ).then_inc(x_loaded[b], 16)

            load_x(0, 0)
            sp.wait_ge(ck_zeroed, 1)
            for g in range(GROUPS):
                sp.dma_start(ck[g * GC:(g + 1) * GC, :, g * GC:(g + 1) * GC],
                             conv_k[:, :, :, g * GC:(g + 1) * GC].rearrange("a b i o -> i (a b) o")
                             ).then_inc(ck_loaded, 16)
            sp.dma_start(bias[:], conv_b.rearrange("(c a) -> c a", a=1)).then_inc(bias_loaded, 16)
            sp.dma_start(rw[:], router_t).then_inc(rw_loaded, 16)
            for e in range(E):
                if e == 2:
                    load_x(1, 1)
                sp.dma_start(ew[:, e], expert_w[:, e]).then_inc(ew_loaded[e], 16)

            def routing(n, b):
                sp.wait_ge(denseT_ready, n + 1)
                sp.sem_inc(passed, 1)
                sp.dma_start(wb_dram[bass.ds(n, 1), :].rearrange("a (r p) -> (a r) p", p=P),
                             denseT[:]).then_inc(wb_out, 16)
                sp.wait_ge(wb_out, 16 * n + 16)
                sp.sem_inc(passed, 1)
                if not isinstance(n, int) or n >= 2:
                    sp.wait_ge(yw_ready, E * (n - 1))
                    sp.sem_inc(passed, 1)
                for q in range(WBQ):
                    lo, hi = q * E * N // WBQ, (q + 1) * E * N // WBQ
                    src = wb_dram[bass.ds(n, 1), lo:hi]
                    sp.dma_start(wb[b][:, q * E // WBQ:(q + 1) * E // WBQ, :].rearrange("p e n -> p (e n)"),
                                 src.broadcast_to([P, hi - lo])).then_inc(wb_loaded[q], 16)

            def store(n, b):
                sp.wait_ge(res_ready, n + 1)
                sp.sem_inc(passed, 1)
                sp.dma_start(out_tok[bass.ds(n, 1)].rearrange("a p t c -> p (a t) c"), res[:]).then_inc(out_stored, 16)

            def chunk(c, b, first=False, last=False, load=True):
                routing(c, b)
                if not first:
                    store(c - 1, 1 - b)
                if load:
                    sp.wait_ge(t_ready, c + 1)
                    sp.sem_inc(passed, 1)
                    load_x(c + 2, b)

            chunk(0, 0, first=True)
            with sp.Fori(0, (chunks - 4) // 2) as i:
                chunk(2 * i + 1, 1)
                chunk(2 * i + 2, 0)
            chunk(chunks - 3, 1)
            chunk(chunks - 2, 0, load=False)
            chunk(chunks - 1, 1, load=False)
            store(chunks - 1, 1)
            sp.wait_ge(out_stored, 16 * chunks)

        @block.tensor
        def _(pe):
            def transposes(dst, src, done):
                for t in range(TT):
                    last = nc.tensor.transpose(dst[:, t * P:(t + 1) * P], src(t), ident[:])
                last.then_inc(done, 1)

            def product(dst, w_hi, w_lo, v_hi, v_lo, start, stop):
                nc.tensor.matmul(dst, w_hi, v_lo, start=start, stop=False)
                nc.tensor.matmul(dst, w_hi, v_hi, start=False, stop=False)
                return nc.tensor.matmul(dst, w_lo, v_hi, start=False, stop=stop)

            def transpose_xn(n):
                pe.wait_ge(xn_ready, n + 1)
                if not isinstance(n, int) or n >= 1:
                    pe.wait_ge(gap_ready, n)
                transposes(ps_a, lambda t: xn[:, t, :], xnT_ready)

            def conv(n, taps):
                if 0 in taps:
                    pe.wait_ge(pad_hi_ready, n + 1)
                    pe.wait_ge(pad_lo_ready, n + 1)
                    if not isinstance(n, int) or n >= 1:
                        pe.wait_ge(denseT_ready, n)
                dst = ps_b[:].rearrange(img, b=IMG, h=HH)
                for k in taps:
                    dy, dx = divmod(k, 3)
                    v_hi = pad_hi[:, :, dy:dy + HH, dx:dx + WW]
                    v_lo = pad_lo[:, :, dy:dy + HH, dx:dx + WW]
                    last = product(dst, ck_hi[:, k, :], ck_lo[:, k, :], v_hi, v_lo, k == 0, k == TAPS - 1)
                if TAPS - 1 in taps:
                    last.then_inc(conv_ready, 1)

            def transpose_relu(n):
                pe.wait_ge(relu_ready, n + 1)
                if not isinstance(n, int) or n >= 2:
                    pe.wait_ge(res_ready, n - 1)
                transposes(ps_a, lambda t: relu[:, t * P:(t + 1) * P], reluT_ready)

            def transpose_zn(n):
                pe.wait_ge(zn_ready, n + 1)
                transposes(ps_b, lambda t: zn[:, t, :], znT_ready)

            def route(n, b):
                pe.wait_ge(z_hi_ready, n + 1)
                pe.wait_ge(z_lo_ready, n + 1)
                for t in range(TT):
                    dst = ps_a[:, t * E:(t + 1) * E]
                    cols = slice(t * P, (t + 1) * P)
                    nc.tensor.matmul(dst, z_lo[b][:, cols], rw_hi[:], start=True, stop=False)
                    nc.tensor.matmul(dst, z_hi[b][:, cols], rw_lo[:], start=False, stop=False)
                    last = nc.tensor.matmul(dst, z_hi[b][:, cols], rw_hi[:], start=False, stop=True)
                last.then_inc(logits_ready, 1)

            def transpose_dense(n):
                pe.wait_ge(dense_ready, n + 1)
                nc.tensor.transpose(ps_b[:, 0:P], dense[:], ident[:]).then_inc(denseT_ps_ready, 1)

            def transpose_acc(n, b):
                pe.wait_ge(acc_ready, E * n + E)
                transposes(ps_a, lambda t: acc[b][:, t * P:(t + 1) * P], accT_ready)

            def gate_up(u, e, j, b, first):
                if first:
                    pe.wait_ge(ew_hi_ready, e + 1)
                    pe.wait_ge(ew_lo_ready, e + 1)
                if not first or e >= 1:
                    pe.wait_ge(sg_ready, 2 * u - 1 + j)
                product(ps_g[j][:], ew_hi[:, e, j, :], ew_lo[:, e, j, :], z_hi[b][:], z_lo[b][:],
                        True, True).then_inc(g_ready, 1)
                if not first or e >= 1:
                    pe.wait_ge(h_ready, 2 * u - 1 + j)
                product(ps_u[j][:], ew_hi[:, e, J + j, :], ew_lo[:, e, J + j, :], z_hi[b][:], z_lo[b][:],
                        True, True).then_inc(u_ready, 1)

            def down(u, e, ub, first=False):
                if not first or e >= 2:
                    pe.wait_ge(yw_ready, u - 1)
                for j in range(J):
                    pe.wait_ge(h_hi_ready, 2 * u + j + 1)
                    pe.wait_ge(h_lo_ready, 2 * u + j + 1)
                    last = product(ps_y[ub][:], ew_hi[:, e, 2 * J + j, :], ew_lo[:, e, 2 * J + j, :],
                                   h_hi[:, ub, j, :], h_lo[:, ub, j, :], j == 0, j == J - 1)
                last.then_inc(y_ready, 1)

            def chunk(c, b, first=False, last=False):
                n = c + 1
                for e in range(E):
                    u = c * E + e
                    gate_up(u, e, 0, b, first)
                    if e == 1 and not last:
                        transpose_xn(n)
                    if e == 4 and not last:
                        transpose_relu(n)
                    gate_up(u, e, 1, b, first)
                    if e == 0:
                        transpose_dense(c)
                    if e == 6 and not last:
                        route(n, 1 - b)
                    if not first or e >= 1:
                        down(u - 1, (e - 1) % E, (e - 1) % 2, first)
                    if e == 2 and not first:
                        transpose_acc(c - 1, 1 - b)
                    if e in (1, 2, 3) and not last:
                        conv(n, range(3 * e - 3, 3 * e))
                    if e == 5 and not last:
                        transpose_zn(n)

            pe.wait_ge(ident_ready, 1)
            transpose_xn(0)
            pe.wait_ge(ck_hi_ready, 1)
            pe.wait_ge(ck_lo_ready, 1)
            conv(0, range(TAPS))
            transpose_relu(0)
            transpose_zn(0)
            pe.wait_ge(rw_hi_ready, 1)
            pe.wait_ge(rw_lo_ready, 1)
            route(0, 0)
            chunk(0, 0, first=True)
            with pe.Fori(0, (chunks - 2) // 2) as i:
                chunk(2 * i + 1, 1)
                chunk(2 * i + 2, 0)
            chunk(chunks - 1, 1, last=True)
            down(chunks * E - 1, E - 1, 1)
            transpose_acc(chunks - 1, 1)

        @block.scalar
        def _(act):
            def pad_heads(n):
                act.wait_ge(xnT_ready, n + 1)
                nc.scalar.copy(pad_hi[:, :, 1:1 + HH, 1:1 + WW],
                               ps_a[:].rearrange(img, b=IMG, h=HH)).then_inc(pad_hi_ready, 1)

            def conv_relu(n):
                act.wait_ge(conv_ready, n + 1)
                if not isinstance(n, int) or n >= 1:
                    act.wait_ge(reluT_ready, n)
                nc.scalar.activation(relu[:], ps_b[:], ACT.Relu, bias=bias[:, 0:1]).then_inc(relu_ready, 1)

            def z_heads(n, b):
                act.wait_ge(znT_ready, n + 1)
                nc.scalar.copy(z_hi[b][:], ps_b[:]).then_inc(z_hi_ready, 1)

            def pair_weight(n):
                act.wait_ge(gap_ready, n + 1)
                nc.scalar.activation(th[:], gap[:], ACT.Tanh, scale=0.5).then_inc(th_ready, 1)

            def dense_rows(n):
                act.wait_ge(denseT_ps_ready, n + 1)
                if not isinstance(n, int) or n >= 1:
                    act.wait_ge(wb_out, 16 * n)
                nc.scalar.copy(denseT[:], ps_b[0:E * TT, 0:P]).then_inc(denseT_ready, 1)

            def chunk(c, b, first=False, last=False):
                n = c + 1
                for e in range(E):
                    u, ub = c * E + e, e % 2
                    if e == 2 and not last:
                        pad_heads(n)
                    if e == 4 and not last:
                        conv_relu(n)
                    if e == 6 and not last:
                        z_heads(n, 1 - b)
                    for j in range(J):
                        act.wait_ge(g_ready, 2 * u + j + 1)
                        if not first or e >= 2:
                            act.wait_ge(h_ready, 2 * u - 3 + j)
                        nc.scalar.activation(sg[:, ub, j, :], ps_g[j][:], ACT.Silu).then_inc(sg_ready, 1)
                    if e == 7 and not last:
                        pair_weight(n)
                    for j in range(J):
                        act.wait_ge(h_ready, 2 * u + j + 1)
                        if not first or e >= 2:
                            act.wait_ge(y_ready, u - 1)
                        nc.scalar.copy(h_hi[:, ub, j, :], hh[:, ub, j, :]).then_inc(h_hi_ready, 1)
                    if e == 0:
                        dense_rows(c)

            act.wait_ge(ck_loaded, 16 * GROUPS)
            nc.scalar.copy(ck_hi[:], ck[:]).then_inc(ck_hi_ready, 1)
            act.wait_ge(consts_ready, 3)
            pad_heads(0)
            act.wait_ge(rw_loaded, 16)
            nc.scalar.copy(rw_hi[:], rw[:]).then_inc(rw_hi_ready, 1)

            def weight_heads(e):
                act.wait_ge(ew_loaded[e], 16)
                nc.scalar.copy(ew_hi[:, e], ew[:, e]).then_inc(ew_hi_ready, 1)

            weight_heads(0)
            weight_heads(1)
            act.wait_ge(bias_loaded, 16)
            conv_relu(0)
            weight_heads(2)
            weight_heads(3)
            weight_heads(4)
            z_heads(0, 0)
            weight_heads(5)
            pair_weight(0)
            weight_heads(6)
            weight_heads(7)
            chunk(0, 0, first=True)
            with act.Fori(0, (chunks - 2) // 2) as i:
                chunk(2 * i + 1, 1)
                chunk(2 * i + 2, 0)
            chunk(chunks - 1, 1, last=True)

        @block.vector
        def _(dve):
            def ln_stats(src, bn, mv, before, done):
                for t in range(TT):
                    nc.vector.bn_stats(bn[:, t, :], src[:, t, :]).then_inc(dve_step, 1)
                dve.wait_ge(dve_step, before + TT)
                dve.sem_inc(passed, 1)
                for t in range(TT):
                    last = nc.vector.bn_aggr(mv[:, t, :], bn[:, t, :])
                last.then_inc(done, 1)

            STEPS = 3 * TT + 5

            def stats_x(n, b):
                dve.wait_ge(x_loaded[b], 8 * n + 16 - 8 * b)
                if not isinstance(n, int) or n >= 1:
                    dve.wait_ge(xn_ready, n)
                ln_stats(xt[b], bn1, mv1, n * STEPS, mv1_ready)

            def pad_tails(n):
                dve.wait_ge(pad_hi_ready, n + 1)
                nc.vector.tensor_tensor(pad_lo[:, :, 1:1 + HH, 1:1 + WW], ps_a[:].rearrange(img, b=IMG, h=HH),
                                        pad_hi[:, :, 1:1 + HH, 1:1 + WW].bitcast(F32), ALU.subtract
                                        ).then_inc(pad_lo_ready, 1)

            def residual(n, b):
                dve.wait_ge(reluT_ready, n + 1)
                nc.vector.tensor_tensor(tt[b][:], ps_a[:].rearrange(tile4, t=TT), xt[b][:], ALU.add).then_inc(t_ready, 1)
                dve.wait_ge(t_ready, n + 1)
                if not isinstance(n, int) or n >= 1:
                    dve.wait_ge(zn_ready, n)
                ln_stats(tt[b], bn2, mv2, n * STEPS + TT, mv2_ready)

            def z_tails(n, b):
                dve.wait_ge(z_hi_ready, n + 1)
                nc.vector.tensor_tensor(z_lo[b][:], ps_b[:], z_hi[b][:].bitcast(F32), ALU.subtract
                                        ).then_inc(z_lo_ready, 1)

            def top_two(n):
                s = n * STEPS + 2 * TT
                dve.wait_ge(logits_ready, n + 1)
                nc.vector.tensor_copy(logits[:], ps_a[:, 0:TT * E].rearrange(tile4, t=TT)).then_inc(dve_step, 1)
                dve.wait_ge(dve_step, s + 1)
                dve.sem_inc(passed, 1)
                for t in range(TT):
                    nc.vector.max(top[:, t, :], logits[:, t, :]).then_inc(dve_step, 1)
                dve.wait_ge(dve_step, s + 1 + TT)
                nc.vector.tensor_tensor(gap[:], top[:, :, 0], top[:, :, 1], ALU.subtract).then_inc(gap_ready, 1)
                for t in range(TT):
                    last = nc.vector.max_index(topi[:, t, :], top[:, t, :], logits[:, t, :])
                last.then_inc(dve_step, 1)

            def dense_weights(n):
                s = n * STEPS + 3 * TT
                dve.wait_ge(th_ready, n + 1)
                nc.vector.tensor_scalar(w12[:, 0, :], th[:], 0.5, 0.5, ALU.mult, ALU.add)
                nc.vector.tensor_scalar(w12[:, 1, :], th[:], -0.5, 0.5, ALU.mult, ALU.add).then_inc(dve_step, 1)
                dve.wait_ge(dve_step, s + 3)
                for k in range(2):
                    last = nc.vector.tensor_tensor(
                        hot[:, k], topi[:, :, k:k + 1].rearrange("p t o -> p o t").broadcast_to([P, E, TT]),
                        iota8[:].rearrange("p (e o) -> p e o", o=1).broadcast_to([P, E, TT]), ALU.is_equal)
                last.then_inc(dve_step, 1)
                dve.wait_ge(dve_step, s + 4)
                for k in range(2):
                    last = nc.vector.tensor_tensor(hot[:, k], hot[:, k],
                                                   w12[:, k:k + 1, :].broadcast_to([P, E, TT]), ALU.mult)
                last.then_inc(dve_step, 1)
                dve.wait_ge(dve_step, s + 5)
                nc.vector.tensor_tensor(dense[:, 0:E * TT], hot[:, 0].rearrange("p e t -> p (e t)"),
                                        hot[:, 1].rearrange("p e t -> p (e t)"), ALU.add).then_inc(dense_ready, 1)

            def weigh(c, b, e, first=False):
                u, ub = c * E + e, e % 2
                if e % (E // WBQ) == 0:
                    dve.wait_ge(wb_loaded[e * WBQ // E], 16 * c + 16)
                dve.wait_ge(y_ready, u + 1)
                if not first or e >= 2:
                    dve.wait_ge(acc_ready, u - 1)
                nc.vector.tensor_tensor(yw[:, ub, :], ps_y[ub][:], wb[b][:, e, :], ALU.mult).then_inc(yw_ready, 1)

            def result(n, b):
                dve.wait_ge(accT_ready, n + 2)
                if not isinstance(n, int) or n >= 1:
                    dve.wait_ge(out_stored, 16 * n)
                nc.vector.tensor_tensor(res[:], ps_a[:].rearrange(tile4, t=TT), tt[b][:], ALU.add).then_inc(res_ready, 1)

            def chunk(c, b, first=False, last=False):
                n = c + 1
                for e in range(E):
                    u, ub = c * E + e, e % 2
                    if e == 0 and not last:
                        stats_x(n, 1 - b)
                    if e == 2 and not last:
                        pad_tails(n)
                    if e == 6 and not last:
                        z_tails(n, 1 - b)
                    if e == 7 and not last:
                        top_two(n)
                    for j in range(J):
                        dve.wait_ge(sg_ready, 2 * u + j + 1)
                        dve.wait_ge(u_ready, 2 * u + j + 1)
                        nc.vector.tensor_tensor(hh[:, ub, j, :], ps_u[j][:], sg[:, ub, j, :], ALU.mult
                                                ).then_inc(h_ready, 1)
                    if e == 4 and not last:
                        residual(n, 1 - b)
                    for j in range(J):
                        dve.wait_ge(h_hi_ready, 2 * u + j + 1)
                        nc.vector.tensor_tensor(h_lo[:, ub, j, :], hh[:, ub, j, :],
                                                h_hi[:, ub, j, :].bitcast(F32), ALU.subtract).then_inc(h_lo_ready, 1)
                    if e == 7 and not last:
                        dense_weights(n)
                    if e >= 1:
                        weigh(c, b, e - 1, first)
                    elif not first:
                        weigh(c - 1, 1 - b, E - 1)
                    if e == 2 and not first:
                        result(c - 1, 1 - b)

            dve.wait_ge(x_loaded[0], 16)
            ln_stats(xt[0], bn1, mv1, 0, mv1_ready)
            dve.wait_ge(ck_loaded, 16 * GROUPS)
            dve.wait_ge(ck_hi_ready, 1)
            nc.vector.tensor_tensor(ck_lo[:], ck[:], ck_hi[:].bitcast(F32), ALU.subtract).then_inc(ck_lo_ready, 1)
            dve.wait_ge(consts_ready, 3)
            pad_tails(0)
            dve.wait_ge(rw_hi_ready, 1)
            nc.vector.tensor_tensor(rw_lo[:], rw[:], rw_hi[:].bitcast(F32), ALU.subtract).then_inc(rw_lo_ready, 1)

            def weight_tails(e):
                dve.wait_ge(ew_hi_ready, e + 1)
                nc.vector.tensor_tensor(ew_lo[:, e], ew[:, e], ew_hi[:, e].bitcast(F32), ALU.subtract
                                        ).then_inc(ew_lo_ready, 1)

            weight_tails(0)
            weight_tails(1)
            residual(0, 0)
            weight_tails(2)
            weight_tails(3)
            z_tails(0, 0)
            weight_tails(4)
            top_two(0)
            weight_tails(5)
            dve.wait_ge(iota_ready, 1)
            dense_weights(0)
            weight_tails(6)
            weight_tails(7)
            chunk(0, 0, first=True)
            with dve.Fori(0, (chunks - 2) // 2) as i:
                chunk(2 * i + 1, 1)
                chunk(2 * i + 2, 0)
            chunk(chunks - 1, 1, last=True)
            weigh(chunks - 1, 1, E - 1)
            result(chunks - 1, 1)

        @block.gpsimd
        def _(pool):
            STEPS = 2 * LINKS_LN

            def normalise(n, src, mv, ln, eps, dst, before, done):
                pool.sem_inc(passed, 1)
                nc.gpsimd.tensor_scalar(ln[:, 0, :], mv[:, :, 1], 1.0, eps, ALU.mult, ALU.add)
                nc.gpsimd.tensor_scalar(ln[:, 2, :], mv[:, :, 0], -1.0, 0.0, ALU.mult, ALU.add).then_inc(pool_step, 1)
                pool.wait_ge(pool_step, before + 1)
                nc.gpsimd.tensor_tensor(ln[:, 1, :], ln[:, 0, :], neghalf[:], ALU.pow).then_inc(pool_step, 1)
                pool.wait_ge(pool_step, before + 2)
                nc.gpsimd.tensor_tensor(ln[:, 3, :], ln[:, 1, :], ln[:, 2, :], ALU.mult).then_inc(pool_step, 1)
                pool.wait_ge(pool_step, before + 3)
                pool.sem_inc(passed, 1)
                for t in range(TT):
                    last = nc.gpsimd.tensor_scalar(dst[:, t, :], src[:, t, :], ln[:, 1, t:t + 1], ln[:, 3, t:t + 1],
                                                   ALU.mult, ALU.add)
                last.then_inc(done, 1)

            def normalise_x(n, b):
                pool.wait_ge(mv1_ready, n + 1)
                if not isinstance(n, int) or n >= 1:
                    pool.wait_ge(xnT_ready, n)
                normalise(n, xt[b], mv1, ln1, EPS_CONV, xn, n * STEPS, xn_ready)

            def normalise_t(n, b):
                pool.wait_ge(mv2_ready, n + 1)
                if not isinstance(n, int) or n >= 1:
                    pool.wait_ge(znT_ready, n)
                normalise(n, tt[b], mv2, ln2, EPS_FFN, zn, n * STEPS + LINKS_LN, zn_ready)

            def accumulate(c, b, e, first=False):
                u, ub = c * E + e, e % 2
                pool.wait_ge(yw_ready, u + 1)
                if e == 0:
                    if not first:
                        pool.wait_ge(accT_ready, c)
                    pool.sem_inc(passed, 1)
                    nc.gpsimd.tensor_copy(acc[b][:], yw[:, ub, :]).then_inc(acc_ready, 1)
                else:
                    pool.wait_ge(acc_ready, u)
                    nc.gpsimd.tensor_tensor(acc[b][:], acc[b][:], yw[:, ub, :], ALU.add).then_inc(acc_ready, 1)

            def chunk(c, b, first=False, last=False):
                n = c + 1
                for e in range(E):
                    if e == 1 and not last:
                        normalise_x(n, 1 - b)
                    if e == 5 and not last:
                        normalise_t(n, 1 - b)
                    if e >= 1:
                        accumulate(c, b, e - 1, first)
                    elif not first:
                        accumulate(c - 1, 1 - b, E - 1)

            nc.gpsimd.memset(ck[:], 0.0).then_inc(ck_zeroed, 1)
            nc.gpsimd.memset(ident[:], 0.0).then_inc(ident_zeroed, 1)
            nc.gpsimd.memset(neghalf[:], -0.5).then_inc(neghalf_ready, 1)
            pool.wait_ge(ident_zeroed, 1)
            nc.gpsimd.affine_select(out=ident[:], in_=ident[:], compare_op=ALU.not_equal, fill=1.0, base=0,
                                    pattern=[[-1, P]], channel_multiplier=1).then_inc(ident_ready, 1)
            pool.wait_ge(neghalf_ready, 1)
            normalise_x(0, 0)
            nc.gpsimd.memset(pad_hi[:].bitcast(F32), 0.0).then_inc(consts_ready, 1)
            nc.gpsimd.memset(pad_lo[:].bitcast(F32), 0.0).then_inc(consts_ready, 1)
            nc.gpsimd.memset(dense[:], 0.0).then_inc(consts_ready, 1)
            nc.gpsimd.iota(iota8[:], pattern=[[1, E]], base=0, channel_multiplier=0,
                           allow_small_or_imprecise_dtypes=True).then_inc(iota_ready, 1)
            normalise_t(0, 0)
            pool.sem_inc(accT_ready, 1)
            chunk(0, 0, first=True)
            with pool.Fori(0, (chunks - 2) // 2) as i:
                chunk(2 * i + 1, 1)
                chunk(2 * i + 2, 0)
            chunk(chunks - 1, 1, last=True)
            accumulate(chunks - 1, 1, E - 1)


def kernel(x, L0_conv_kernel, L0_conv_bias, L0_ffn_router_w, L0_ffn_w_gate, L0_ffn_w_up, L0_ffn_w_down):
    import concourse.bacc as bacc
    from concourse.bass_utils import run_bass_kernel_spmd

    gate, up, down = (np.asarray(w) for w in (L0_ffn_w_gate, L0_ffn_w_up, L0_ffn_w_down))
    arrays = {
        "x": np.asarray(x),
        "conv_k": np.asarray(L0_conv_kernel),
        "conv_b": np.asarray(L0_conv_bias),
        "router_t": np.asarray(L0_ffn_router_w).T,
        "expert_w": np.concatenate(
            [w.reshape(E, P, J, P).transpose(1, 0, 2, 3) for w in (gate, up)]
            + [down.reshape(E, J, P, P).transpose(2, 0, 1, 3)], axis=2),
    }
    arrays = {k: np.ascontiguousarray(a) for k, a in arrays.items()}
    nc = bacc.Bacc("TRN2", target_bir_lowering=False, num_devices=1)
    args = [nc.dram_tensor(k, a.shape, mybir.dt.from_np(a.dtype), kind="ExternalInput").ap()
            for k, a in arrays.items()]
    out = nc.dram_tensor("out", arrays["x"].shape, F32, kind="ExternalOutput").ap()
    metaformer_moe(nc, *args, out)
    return run_bass_kernel_spmd(nc, [arrays], core_ids=[0]).results[0]["out"]
```

```python
from contextlib import ExitStack

import numpy as np

import concourse.bass as bass
from concourse import mybir

ALU = mybir.AluOpType
ACT = mybir.ActivationFunctionType
F32 = mybir.dt.float32
F32R = mybir.dt.float32r
U32 = mybir.dt.uint32

P = 128
IMG, HH, WW = 2, 16, 16
N = IMG * HH * WW
TT = N // P
E = 8
J = 2
TAPS = 9
GROUPS = 8
GC = P // GROUPS
EPS_CONV, EPS_FFN = 1e-6, 1e-5
WBQ = 4


def metaformer_moe(nc, x, conv_k, conv_b, router_t, expert_w, out):
    chunks = x.shape[0] // IMG
    x_tok = x.rearrange("b h w c -> (b h w) c").rearrange("(n t p) c -> n p t c", t=TT, p=P)
    out_tok = out.rearrange("b h w c -> (b h w) c").rearrange("(n t p) c -> n p t c", t=TT, p=P)
    wb_dram = nc.dram_tensor("wb_dram", [chunks, E * N], F32, kind="Internal").ap()

    with ExitStack() as ctx:
        def sb(name, shape, dt=F32):
            return ctx.enter_context(nc.sbuf_tensor(name, shape, dt))

        def sem(name):
            return ctx.enter_context(nc.semaphore(name))

        ident = sb("ident", [P, P])
        iota8 = sb("iota8", [P, E])
        neghalf = sb("neghalf", [P, TT])
        bias = sb("bias", [P, 1])
        ck = sb("ck", [P, TAPS, GC])
        ckc_hi, ckc_lo = sb("ckc_hi", [P, TAPS, GC], F32R), sb("ckc_lo", [P, TAPS, GC])
        own = sb("own", [P, GROUPS, GC])
        ck_hi, ck_lo = sb("ck_hi", [P, TAPS, P], F32R), sb("ck_lo", [P, TAPS, P], F32R)
        rw = sb("rw", [P, E])
        rw_hi, rw_lo = sb("rw_hi", [P, E], F32R), sb("rw_lo", [P, E], F32R)
        ew = sb("ew", [P, E, 3 * J, P])
        ew_hi, ew_lo = sb("ew_hi", [P, E, 3 * J, P], F32R), sb("ew_lo", [P, E, 3 * J, P], F32R)
        xt = [sb(f"xt{b}", [P, TT, P]) for b in range(2)]
        xn = sb("xn", [P, TT, P])
        pad_hi = sb("pad_hi", [P, IMG, HH + 2, WW + 2], F32R)
        pad_lo = sb("pad_lo", [P, IMG, HH + 2, WW + 2], F32R)
        relu = sb("relu", [P, N])
        tt = [sb(f"tt{b}", [P, TT, P]) for b in range(2)]
        zn = sb("zn", [P, TT, P])
        z_hi = [sb(f"z_hi{b}", [P, N], F32R) for b in range(2)]
        z_lo = [sb(f"z_lo{b}", [P, N], F32R) for b in range(2)]
        bn1, bn2 = sb("bn1", [P, TT, 6]), sb("bn2", [P, TT, 6])
        mv1, mv2 = sb("mv1", [P, TT, 2]), sb("mv2", [P, TT, 2])
        ve1, ve2 = sb("ve1", [P, TT]), sb("ve2", [P, TT])
        rstd1, rstd2 = sb("rstd1", [P, TT]), sb("rstd2", [P, TT])
        logits = sb("logits", [P, TT, E])
        top = sb("top", [P, TT, E])
        topi = sb("topi", [P, TT, E], U32)
        gap = sb("gap", [P, TT])
        th = sb("th", [P, TT])
        w12 = sb("w12", [P, 2, TT])
        hot = sb("hot", [P, 2, E, TT])
        dense = sb("dense", [P, P])
        denseT = sb("denseT", [E * TT, P])
        wb = [sb(f"wb{b}", [P, E, N]) for b in range(2)]
        sg = sb("sg", [P, 2, J, N])
        hh = sb("hh", [P, 2, J, N])
        h_hi, h_lo = sb("h_hi", [P, 2, J, N], F32R), sb("h_lo", [P, 2, J, N], F32R)
        yw = sb("yw", [P, 2, N])
        acc = [sb(f"acc{b}", [P, N]) for b in range(2)]
        res = sb("res", [P, TT, P])

        ps_g = [ctx.enter_context(nc.psum_tensor(f"ps_g{j}", [P, N], F32)) for j in range(J)]
        ps_u = [ctx.enter_context(nc.psum_tensor(f"ps_u{j}", [P, N], F32)) for j in range(J)]
        ps_y = [ctx.enter_context(nc.psum_tensor(f"ps_y{b}", [P, N], F32)) for b in range(2)]
        ps_a = ctx.enter_context(nc.psum_tensor("ps_a", [P, N], F32))
        ps_b = ctx.enter_context(nc.psum_tensor("ps_b", [P, N], F32))

        x_loaded = [sem(f"x_loaded{b}") for b in range(2)]
        ck_loaded, bias_loaded, rw_loaded = sem("ck_loaded"), sem("bias_loaded"), sem("rw_loaded")
        ew_loaded = [sem(f"ew_loaded{q}") for q in range(E)]
        wb_out, out_stored = sem("wb_out"), sem("out_stored")
        wb_loaded = [sem(f"wb_loaded{q}") for q in range(WBQ)]
        ident_zeroed, ident_ready, consts_ready, own_ready = (
            sem("ident_zeroed"), sem("ident_ready"), sem("consts_ready"), sem("own_ready"))
        ckc_hi_ready, ckc_lo_ready = sem("ckc_hi_ready"), sem("ckc_lo_ready")
        neghalf_ready, iota_ready = sem("neghalf_ready"), sem("iota_ready")
        ck_hi_ready, ck_lo_ready = sem("ck_hi_ready"), sem("ck_lo_ready")
        rw_hi_ready, rw_lo_ready = sem("rw_hi_ready"), sem("rw_lo_ready")
        ew_hi_ready, ew_lo_ready = sem("ew_hi_ready"), sem("ew_lo_ready")
        mv1_ready, xn_ready, xnT_ready = sem("mv1_ready"), sem("xn_ready"), sem("xnT_ready")
        rstd1_ready, rstd2_ready = sem("rstd1_ready"), sem("rstd2_ready")
        pad_hi_ready, pad_lo_ready, conv_ready = sem("pad_hi_ready"), sem("pad_lo_ready"), sem("conv_ready")
        relu_ready, reluT_ready, t_ready = sem("relu_ready"), sem("reluT_ready"), sem("t_ready")
        mv2_ready, zn_ready, znT_ready = sem("mv2_ready"), sem("zn_ready"), sem("znT_ready")
        z_hi_ready, z_lo_ready, logits_ready = sem("z_hi_ready"), sem("z_lo_ready"), sem("logits_ready")
        gap_ready, th_ready, dense_ready = sem("gap_ready"), sem("th_ready"), sem("dense_ready")
        denseT_ps_ready, denseT_ready = sem("denseT_ps_ready"), sem("denseT_ready")
        passed = sem("passed")
        dve_step, pool_step = sem("dve_step"), sem("pool_step")
        g_ready, u_ready, sg_ready, h_ready = sem("g_ready"), sem("u_ready"), sem("sg_ready"), sem("h_ready")
        h_hi_ready, h_lo_ready, y_ready = sem("h_hi_ready"), sem("h_lo_ready"), sem("y_ready")
        yw_ready, acc_ready, accT_ready, res_ready = sem("yw_ready"), sem("acc_ready"), sem("accT_ready"), sem("res_ready")

        img = "p (b h w) -> p b h w"
        tile4 = "p (t c) -> p t c"

        block = ctx.enter_context(nc.Block())

        @block.sync
        def _(sp):
            def load_x(n, b):
                sp.dma_start(xt[b][:], x_tok[bass.ds(n, 1)].rearrange("a p t c -> p (a t) c")
                             ).then_inc(x_loaded[b], 16)

            load_x(0, 0)
            for e in range(E):
                if e == 2:
                    load_x(1, 1)
                sp.dma_start(ew[:, e], expert_w[:, e]).then_inc(ew_loaded[e], 16)

            def routing(n, b):
                sp.wait_ge(denseT_ready, n + 1)
                sp.sem_inc(passed, 1)
                sp.dma_start(wb_dram[bass.ds(n, 1), :].rearrange("a (r p) -> (a r) p", p=P),
                             denseT[:]).then_inc(wb_out, 16)
                sp.wait_ge(wb_out, 16 * n + 16)
                sp.sem_inc(passed, 1)
                if not isinstance(n, int) or n >= 2:
                    sp.wait_ge(yw_ready, E * (n - 1))
                    sp.sem_inc(passed, 1)
                for q in range(WBQ):
                    lo, hi = q * E * N // WBQ, (q + 1) * E * N // WBQ
                    src = wb_dram[bass.ds(n, 1), lo:hi]
                    sp.dma_start(wb[b][:, q * E // WBQ:(q + 1) * E // WBQ, :].rearrange("p e n -> p (e n)"),
                                 src.broadcast_to([P, hi - lo])).then_inc(wb_loaded[q], 16)

            def store(n, b):
                sp.wait_ge(res_ready, n + 1)
                sp.sem_inc(passed, 1)
                sp.dma_start(out_tok[bass.ds(n, 1)].rearrange("a p t c -> p (a t) c"), res[:]).then_inc(out_stored, 16)

            def chunk(c, b, first=False, last=False, load=True):
                routing(c, b)
                if not first:
                    store(c - 1, 1 - b)
                if load:
                    sp.wait_ge(t_ready, c + 1)
                    sp.sem_inc(passed, 1)
                    load_x(c + 2, b)

            chunk(0, 0, first=True)
            with sp.Fori(0, (chunks - 4) // 2) as i:
                chunk(2 * i + 1, 1)
                chunk(2 * i + 2, 0)
            chunk(chunks - 3, 1)
            chunk(chunks - 2, 0, load=False)
            chunk(chunks - 1, 1, load=False)
            store(chunks - 1, 1)
            sp.wait_ge(out_stored, 16 * chunks)

        @block.tensor
        def _(pe):
            def transposes(dst, src, done):
                for t in range(TT):
                    last = nc.tensor.transpose(dst[:, t * P:(t + 1) * P], src(t), ident[:])
                last.then_inc(done, 1)

            def product(dst, w_hi, w_lo, v_hi, v_lo, start, stop):
                nc.tensor.matmul(dst, w_hi, v_lo, start=start, stop=False)
                nc.tensor.matmul(dst, w_hi, v_hi, start=False, stop=False)
                return nc.tensor.matmul(dst, w_lo, v_hi, start=False, stop=stop)

            def transpose_xn(n):
                pe.wait_ge(xn_ready, n + 1)
                if not isinstance(n, int) or n >= 1:
                    pe.wait_ge(gap_ready, n)
                transposes(ps_a, lambda t: xn[:, t, :], xnT_ready)

            def conv(n):
                pe.wait_ge(pad_hi_ready, n + 1)
                pe.wait_ge(pad_lo_ready, n + 1)
                if not isinstance(n, int) or n >= 1:
                    pe.wait_ge(denseT_ready, n)
                dst = ps_b[:].rearrange(img, b=IMG, h=HH)
                for k in range(TAPS):
                    dy, dx = divmod(k, 3)
                    v_hi = pad_hi[:, :, dy:dy + HH, dx:dx + WW]
                    v_lo = pad_lo[:, :, dy:dy + HH, dx:dx + WW]
                    last = product(dst, ck_hi[:, k, :], ck_lo[:, k, :], v_hi, v_lo, k == 0, k == TAPS - 1)
                last.then_inc(conv_ready, 1)

            def transpose_relu(n):
                pe.wait_ge(relu_ready, n + 1)
                if not isinstance(n, int) or n >= 2:
                    pe.wait_ge(res_ready, n - 1)
                transposes(ps_a, lambda t: relu[:, t * P:(t + 1) * P], reluT_ready)

            def transpose_zn(n):
                pe.wait_ge(zn_ready, n + 1)
                transposes(ps_b, lambda t: zn[:, t, :], znT_ready)

            def route(n, b):
                pe.wait_ge(z_hi_ready, n + 1)
                pe.wait_ge(z_lo_ready, n + 1)
                for t in range(TT):
                    dst = ps_a[:, t * E:(t + 1) * E]
                    cols = slice(t * P, (t + 1) * P)
                    nc.tensor.matmul(dst, z_lo[b][:, cols], rw_hi[:], start=True, stop=False)
                    nc.tensor.matmul(dst, z_hi[b][:, cols], rw_lo[:], start=False, stop=False)
                    last = nc.tensor.matmul(dst, z_hi[b][:, cols], rw_hi[:], start=False, stop=True)
                last.then_inc(logits_ready, 1)

            def transpose_dense(n):
                pe.wait_ge(dense_ready, n + 1)
                nc.tensor.transpose(ps_b[:, 0:P], dense[:], ident[:]).then_inc(denseT_ps_ready, 1)

            def transpose_acc(n, b):
                pe.wait_ge(acc_ready, (E - 1) * (n + 1))
                transposes(ps_a, lambda t: acc[b][:, t * P:(t + 1) * P], accT_ready)

            def gate_up(u, e, j, b, first):
                if first:
                    pe.wait_ge(ew_hi_ready, e + 1)
                    pe.wait_ge(ew_lo_ready, e + 1)
                if not first or e >= 1:
                    pe.wait_ge(sg_ready, 2 * u - 1 + j)
                product(ps_g[j][:], ew_hi[:, e, j, :], ew_lo[:, e, j, :], z_hi[b][:], z_lo[b][:],
                        True, True).then_inc(g_ready, 1)
                if not first or e >= 1:
                    pe.wait_ge(h_ready, 2 * u - 1 + j)
                product(ps_u[j][:], ew_hi[:, e, J + j, :], ew_lo[:, e, J + j, :], z_hi[b][:], z_lo[b][:],
                        True, True).then_inc(u_ready, 1)

            def down(u, e, ub, first=False):
                if not first or e >= 2:
                    pe.wait_ge(yw_ready, u - 1)
                for j in range(J):
                    pe.wait_ge(h_hi_ready, 2 * u + j + 1)
                    pe.wait_ge(h_lo_ready, 2 * u + j + 1)
                    last = product(ps_y[ub][:], ew_hi[:, e, 2 * J + j, :], ew_lo[:, e, 2 * J + j, :],
                                   h_hi[:, ub, j, :], h_lo[:, ub, j, :], j == 0, j == J - 1)
                last.then_inc(y_ready, 1)

            def chunk(c, b, first=False, last=False):
                n = c + 1
                for e in range(E):
                    u = c * E + e
                    gate_up(u, e, 0, b, first)
                    if e == 0:
                        transpose_dense(c)
                    if e == 3 and not last:
                        transpose_relu(n)
                    if e == 5 and not last:
                        transpose_zn(n)
                    if e == 6 and not last:
                        route(n, 1 - b)
                    gate_up(u, e, 1, b, first)
                    if not first or e >= 1:
                        down(u - 1, (e - 1) % E, (e - 1) % 2, first)
                    if e == 1 and not last:
                        transpose_xn(n)
                    if e == 2 and not last:
                        conv(n)
                    if e == 2 and not first:
                        transpose_acc(c - 1, 1 - b)

            pe.wait_ge(ident_ready, 1)
            def keep_warm(times):
                for _ in range(times):
                    nc.tensor.matmul(ps_y[0][:, 0:P], ident[:], ident[:], start=True, stop=True)

            keep_warm(12)
            transpose_xn(0)
            keep_warm(4)
            pe.wait_ge(ck_hi_ready, 1)
            pe.wait_ge(ck_lo_ready, 1)
            conv(0)
            transpose_relu(0)
            keep_warm(16)
            transpose_zn(0)
            keep_warm(4)
            pe.wait_ge(rw_hi_ready, 1)
            pe.wait_ge(rw_lo_ready, 1)
            route(0, 0)
            chunk(0, 0, first=True)
            with pe.Fori(0, (chunks - 2) // 2) as i:
                chunk(2 * i + 1, 1)
                chunk(2 * i + 2, 0)
            chunk(chunks - 1, 1, last=True)
            down(chunks * E - 1, E - 1, 1)
            transpose_acc(chunks - 1, 1)

        @block.scalar
        def _(act):
            def pad_heads(n):
                act.wait_ge(xnT_ready, n + 1)
                nc.scalar.copy(pad_hi[:, :, 1:1 + HH, 1:1 + WW],
                               ps_a[:].rearrange(img, b=IMG, h=HH)).then_inc(pad_hi_ready, 1)

            def conv_relu(n):
                act.wait_ge(conv_ready, n + 1)
                if not isinstance(n, int) or n >= 1:
                    act.wait_ge(reluT_ready, n)
                nc.scalar.activation(relu[:], ps_b[:], ACT.Relu, bias=bias[:, 0:1]).then_inc(relu_ready, 1)

            def z_heads(n, b):
                act.wait_ge(znT_ready, n + 1)
                nc.scalar.copy(z_hi[b][:], ps_b[:]).then_inc(z_hi_ready, 1)

            def pair_weight(n):
                act.wait_ge(gap_ready, n + 1)
                nc.scalar.activation(th[:], gap[:], ACT.Tanh, scale=0.5).then_inc(th_ready, 1)

            def dense_rows(n):
                act.wait_ge(denseT_ps_ready, n + 1)
                if not isinstance(n, int) or n >= 1:
                    act.wait_ge(wb_out, 16 * n)
                nc.scalar.copy(denseT[:], ps_b[0:E * TT, 0:P]).then_inc(denseT_ready, 1)

            def chunk(c, b, first=False, last=False):
                n = c + 1
                for e in range(E):
                    u, ub = c * E + e, e % 2
                    if e == 3 and not last:
                        conv_relu(n)
                    for j in range(J):
                        act.wait_ge(g_ready, 2 * u + j + 1)
                        if not first or e >= 2:
                            act.wait_ge(h_ready, 2 * u - 3 + j)
                        nc.scalar.activation(sg[:, ub, j, :], ps_g[j][:], ACT.Silu).then_inc(sg_ready, 1)
                        if e == 0 and j == 0:
                            dense_rows(c)
                        if e == 2 and j == 0 and not last:
                            pad_heads(n)
                        if e == 5 and j == 0 and not last:
                            z_heads(n, 1 - b)
                    for j in range(J):
                        act.wait_ge(h_ready, 2 * u + j + 1)
                        if not first or e >= 2:
                            act.wait_ge(y_ready, u - 1)
                        nc.scalar.copy(h_hi[:, ub, j, :], hh[:, ub, j, :]).then_inc(h_hi_ready, 1)
                    if e == 6 and not last:
                        pair_weight(n)

            act.dma_start(ck[:], conv_k).then_inc(ck_loaded, 16)
            act.dma_start(bias[:], conv_b.rearrange("(c a) -> c a", a=1)).then_inc(bias_loaded, 16)
            act.dma_start(rw[:], router_t).then_inc(rw_loaded, 16)
            act.wait_ge(neghalf_ready, 1)
            nc.scalar.activation(th[:], neghalf[:], ACT.Silu)
            act.wait_ge(ck_loaded, 16)
            nc.scalar.copy(ckc_hi[:], ck[:]).then_inc(ckc_hi_ready, 1)
            act.wait_ge(consts_ready, 3)
            pad_heads(0)
            act.wait_ge(rw_loaded, 16)
            nc.scalar.copy(rw_hi[:], rw[:]).then_inc(rw_hi_ready, 1)

            def weight_heads(e):
                act.wait_ge(ew_loaded[e], 16)
                nc.scalar.copy(ew_hi[:, e], ew[:, e]).then_inc(ew_hi_ready, 1)

            for e in (0, 1, 2, 3):
                weight_heads(e)
            act.wait_ge(bias_loaded, 16)
            conv_relu(0)
            weight_heads(4)
            weight_heads(5)
            z_heads(0, 0)
            weight_heads(6)
            pair_weight(0)
            weight_heads(7)
            chunk(0, 0, first=True)
            with act.Fori(0, (chunks - 2) // 2) as i:
                chunk(2 * i + 1, 1)
                chunk(2 * i + 2, 0)
            chunk(chunks - 1, 1, last=True)

        @block.vector
        def _(dve):
            def ln_stats(src, bn, mv, before, done):
                for t in range(TT):
                    nc.vector.bn_stats(bn[:, t, :], src[:, t, :]).then_inc(dve_step, 1)
                dve.wait_ge(dve_step, before + TT)
                dve.sem_inc(passed, 1)
                for t in range(TT):
                    last = nc.vector.bn_aggr(mv[:, t, :], bn[:, t, :])
                last.then_inc(done, 1)

            def ln_apply(src, mv, rstd, dst, done):
                for t in range(TT):
                    last = nc.vector.tensor_scalar(dst[:, t, :], src[:, t, :], mv[:, t, 0:1], rstd[:, t:t + 1],
                                                   ALU.subtract, ALU.mult)
                last.then_inc(done, 1)

            def normalise_x(n, b):
                dve.wait_ge(rstd1_ready, n + 1)
                if not isinstance(n, int) or n >= 1:
                    dve.wait_ge(xnT_ready, n)
                ln_apply(xt[b], mv1, rstd1, xn, xn_ready)

            def normalise_t(n, b):
                dve.wait_ge(rstd2_ready, n + 1)
                if not isinstance(n, int) or n >= 1:
                    dve.wait_ge(znT_ready, n)
                ln_apply(tt[b], mv2, rstd2, zn, zn_ready)

            STEPS = 3 * TT + 5

            def stats_x(n, b):
                dve.wait_ge(x_loaded[b], 8 * n + 16 - 8 * b)
                ln_stats(xt[b], bn1, mv1, n * STEPS, mv1_ready)

            def pad_tails(n):
                dve.wait_ge(pad_hi_ready, n + 1)
                nc.vector.tensor_tensor(pad_lo[:, :, 1:1 + HH, 1:1 + WW], ps_a[:].rearrange(img, b=IMG, h=HH),
                                        pad_hi[:, :, 1:1 + HH, 1:1 + WW].bitcast(F32), ALU.subtract
                                        ).then_inc(pad_lo_ready, 1)

            def residual(n, b):
                dve.wait_ge(reluT_ready, n + 1)
                nc.vector.tensor_tensor(tt[b][:], ps_a[:].rearrange(tile4, t=TT), xt[b][:], ALU.add).then_inc(t_ready, 1)
                dve.wait_ge(t_ready, n + 1)
                ln_stats(tt[b], bn2, mv2, n * STEPS + TT, mv2_ready)

            def z_tails(n, b):
                dve.wait_ge(z_hi_ready, n + 1)
                nc.vector.tensor_tensor(z_lo[b][:], ps_b[:], z_hi[b][:].bitcast(F32), ALU.subtract
                                        ).then_inc(z_lo_ready, 1)

            def top_two(n):
                s = n * STEPS + 2 * TT
                dve.wait_ge(logits_ready, n + 1)
                nc.vector.tensor_copy(logits[:], ps_a[:, 0:TT * E].rearrange(tile4, t=TT)).then_inc(dve_step, 1)
                dve.wait_ge(dve_step, s + 1)
                dve.sem_inc(passed, 1)
                for t in range(TT):
                    nc.vector.max(top[:, t, :], logits[:, t, :]).then_inc(dve_step, 1)
                dve.wait_ge(dve_step, s + 1 + TT)
                nc.vector.tensor_tensor(gap[:], top[:, :, 0], top[:, :, 1], ALU.subtract).then_inc(gap_ready, 1)
                for t in range(TT):
                    last = nc.vector.max_index(topi[:, t, :], top[:, t, :], logits[:, t, :])
                last.then_inc(dve_step, 1)
                dve.wait_ge(dve_step, s + 2 + TT)
                for k in range(2):
                    last = nc.vector.tensor_tensor(
                        hot[:, k], topi[:, :, k:k + 1].rearrange("p t o -> p o t").broadcast_to([P, E, TT]),
                        iota8[:].rearrange("p (e o) -> p e o", o=1).broadcast_to([P, E, TT]), ALU.is_equal)
                last.then_inc(dve_step, 1)

            def dense_weights(n):
                s = n * STEPS + 3 * TT
                dve.wait_ge(th_ready, n + 1)
                nc.vector.tensor_scalar(w12[:, 0, :], th[:], 0.5, 0.5, ALU.mult, ALU.add)
                nc.vector.tensor_scalar(w12[:, 1, :], th[:], -0.5, 0.5, ALU.mult, ALU.add).then_inc(dve_step, 1)
                dve.wait_ge(dve_step, s + 4)
                for k in range(2):
                    last = nc.vector.tensor_tensor(hot[:, k], hot[:, k],
                                                   w12[:, k:k + 1, :].broadcast_to([P, E, TT]), ALU.mult)
                last.then_inc(dve_step, 1)
                dve.wait_ge(dve_step, s + 5)
                nc.vector.tensor_tensor(dense[:, 0:E * TT], hot[:, 0].rearrange("p e t -> p (e t)"),
                                        hot[:, 1].rearrange("p e t -> p (e t)"), ALU.add).then_inc(dense_ready, 1)

            def weigh(c, b, e, first=False):
                u, ub = c * E + e, e % 2
                if e % (E // WBQ) == 0:
                    dve.wait_ge(wb_loaded[e * WBQ // E], 16 * c + 16)
                dve.wait_ge(y_ready, u + 1)
                if e == 0 and not first:
                    dve.wait_ge(accT_ready, c)
                if e == 1 and not first:
                    dve.wait_ge(acc_ready, (E - 1) * c)
                if e >= 3:
                    dve.wait_ge(acc_ready, (E - 1) * c + e - 2)
                dst = acc[b][:] if e == 0 else yw[:, ub, :]
                nc.vector.tensor_tensor(dst, ps_y[ub][:], wb[b][:, e, :], ALU.mult).then_inc(yw_ready, 1)

            def result(n, b):
                dve.wait_ge(accT_ready, n + 2)
                if not isinstance(n, int) or n >= 1:
                    dve.wait_ge(out_stored, 16 * n)
                nc.vector.tensor_tensor(res[:], ps_a[:].rearrange(tile4, t=TT), tt[b][:], ALU.add).then_inc(res_ready, 1)

            def chunk(c, b, first=False, last=False):
                n = c + 1
                for e in range(E):
                    u, ub = c * E + e, e % 2
                    if e == 3 and not first:
                        result(c - 1, 1 - b)
                    for j in range(J):
                        dve.wait_ge(sg_ready, 2 * u + j + 1)
                        dve.wait_ge(u_ready, 2 * u + j + 1)
                        nc.vector.tensor_tensor(hh[:, ub, j, :], ps_u[j][:], sg[:, ub, j, :], ALU.mult
                                                ).then_inc(h_ready, 1)
                        if e == 0 and j == 0 and not last:
                            stats_x(n, 1 - b)
                        if e == 2 and j == 0 and not last:
                            pad_tails(n)
                    if e == 4 and not last:
                        normalise_t(n, 1 - b)
                    if e == 5 and not last:
                        z_tails(n, 1 - b)
                    if e == 7 and not last:
                        dense_weights(n)
                    for j in range(J):
                        dve.wait_ge(h_hi_ready, 2 * u + j + 1)
                        nc.vector.tensor_tensor(h_lo[:, ub, j, :], hh[:, ub, j, :],
                                                h_hi[:, ub, j, :].bitcast(F32), ALU.subtract).then_inc(h_lo_ready, 1)
                    if e == 0 and not last:
                        normalise_x(n, 1 - b)
                    if e == 3 and not last:
                        residual(n, 1 - b)
                    if e == 6 and not last:
                        top_two(n)
                    if e >= 1:
                        weigh(c, b, e - 1, first)
                    elif not first:
                        weigh(c - 1, 1 - b, E - 1)

            dve.wait_ge(x_loaded[0], 16)
            ln_stats(xt[0], bn1, mv1, 0, mv1_ready)
            def spread(dst, src, done):
                nc.vector.tensor_tensor(
                    dst[:].rearrange("p k (g o) -> p k g o", g=GROUPS),
                    src.rearrange("p k (g o) -> p k g o", g=1).broadcast_to([P, TAPS, GROUPS, GC]),
                    own[:].rearrange("p (k g) o -> p k g o", k=1).broadcast_to([P, TAPS, GROUPS, GC]),
                    ALU.mult).then_inc(done, 1)

            dve.wait_ge(ckc_hi_ready, 1)
            nc.vector.tensor_tensor(ckc_lo[:], ck[:], ckc_hi[:].bitcast(F32), ALU.subtract).then_inc(ckc_lo_ready, 1)
            dve.wait_ge(own_ready, 3)
            spread(ck_hi, ckc_hi[:].bitcast(F32), ck_hi_ready)
            normalise_x(0, 0)
            dve.wait_ge(ckc_lo_ready, 1)
            spread(ck_lo, ckc_lo[:], ck_lo_ready)
            dve.wait_ge(consts_ready, 3)
            pad_tails(0)
            dve.wait_ge(rw_hi_ready, 1)
            nc.vector.tensor_tensor(rw_lo[:], rw[:], rw_hi[:].bitcast(F32), ALU.subtract).then_inc(rw_lo_ready, 1)

            residual(0, 0)
            normalise_t(0, 0)
            z_tails(0, 0)
            dve.wait_ge(iota_ready, 1)
            top_two(0)
            dense_weights(0)
            chunk(0, 0, first=True)
            with dve.Fori(0, (chunks - 2) // 2) as i:
                chunk(2 * i + 1, 1)
                chunk(2 * i + 2, 0)
            chunk(chunks - 1, 1, last=True)
            weigh(chunks - 1, 1, E - 1)
            result(chunks - 1, 1)

        @block.gpsimd
        def _(pool):
            STEPS = 2

            def inverse_std(mv, eps, ve, rstd, before, done):
                pool.sem_inc(passed, 1)
                nc.gpsimd.tensor_scalar(ve[:], mv[:, :, 1], 1.0, eps, ALU.mult, ALU.add).then_inc(pool_step, 1)
                pool.wait_ge(pool_step, before + 1)
                nc.gpsimd.tensor_tensor(rstd[:], ve[:], neghalf[:], ALU.pow).then_inc(done, 1)

            def rstd_x(n):
                pool.wait_ge(mv1_ready, n + 1)
                inverse_std(mv1, EPS_CONV, ve1, rstd1, n * STEPS, rstd1_ready)

            def rstd_t(n):
                pool.wait_ge(mv2_ready, n + 1)
                inverse_std(mv2, EPS_FFN, ve2, rstd2, n * STEPS + 1, rstd2_ready)

            def accumulate(c, b, e):
                pool.wait_ge(yw_ready, c * E + e + 1)
                if e >= 2:
                    pool.wait_ge(acc_ready, (E - 1) * c + e - 1)
                nc.gpsimd.tensor_tensor(acc[b][:], acc[b][:], yw[:, e % 2, :], ALU.add).then_inc(acc_ready, 1)

            def chunk(c, b, first=False, last=False):
                n = c + 1
                for e in range(E):
                    if e == 0 and not last:
                        rstd_x(n)
                    if e == 3 and not last:
                        rstd_t(n)
                    if e >= 2:
                        accumulate(c, b, e - 1)
                    if e == 0 and not first:
                        accumulate(c - 1, 1 - b, E - 1)

            def weight_tails(e):
                pool.wait_ge(ew_hi_ready, e + 1)
                nc.gpsimd.tensor_tensor(ew_lo[:, e], ew[:, e], ew_hi[:, e].bitcast(F32), ALU.subtract
                                        ).then_inc(ew_lo_ready, 1)

            nc.gpsimd.memset(ident[:], 0.0).then_inc(ident_zeroed, 1)
            nc.gpsimd.memset(neghalf[:], -0.5).then_inc(neghalf_ready, 1)
            pool.wait_ge(ident_zeroed, 1)
            nc.gpsimd.affine_select(out=ident[:], in_=ident[:], compare_op=ALU.not_equal, fill=1.0, base=0,
                                    pattern=[[-1, P]], channel_multiplier=1).then_inc(ident_ready, 1)
            nc.gpsimd.memset(own[:], 1.0).then_inc(own_ready, 1)
            pool.wait_ge(own_ready, 1)
            nc.gpsimd.affine_select(out=own[:], in_=own[:], compare_op=ALU.is_ge, fill=0.0, base=0,
                                    pattern=[[-GC, GROUPS], [0, GC]], channel_multiplier=1).then_inc(own_ready, 1)
            pool.wait_ge(own_ready, 2)
            nc.gpsimd.affine_select(out=own[:], in_=own[:], compare_op=ALU.is_ge, fill=0.0, base=GC - 1,
                                    pattern=[[GC, GROUPS], [0, GC]], channel_multiplier=-1).then_inc(own_ready, 1)
            pool.wait_ge(neghalf_ready, 1)
            rstd_x(0)
            nc.gpsimd.memset(pad_hi[:].bitcast(F32), 0.0).then_inc(consts_ready, 1)
            nc.gpsimd.memset(pad_lo[:].bitcast(F32), 0.0).then_inc(consts_ready, 1)
            nc.gpsimd.memset(dense[:], 0.0).then_inc(consts_ready, 1)
            nc.gpsimd.iota(iota8[:], pattern=[[1, E]], base=0, channel_multiplier=0,
                           allow_small_or_imprecise_dtypes=True).then_inc(iota_ready, 1)
            for e in (0, 1, 2):
                weight_tails(e)
            rstd_t(0)
            for e in range(3, E):
                weight_tails(e)
            pool.sem_inc(accT_ready, 1)
            chunk(0, 0, first=True)
            with pool.Fori(0, (chunks - 2) // 2) as i:
                chunk(2 * i + 1, 1)
                chunk(2 * i + 2, 0)
            chunk(chunks - 1, 1, last=True)
            accumulate(chunks - 1, 1, E - 1)


def kernel(x, L0_conv_kernel, L0_conv_bias, L0_ffn_router_w, L0_ffn_w_gate, L0_ffn_w_up, L0_ffn_w_down):
    import concourse.bacc as bacc
    from concourse.bass_utils import run_bass_kernel_spmd

    gate, up, down = (np.asarray(w) for w in (L0_ffn_w_gate, L0_ffn_w_up, L0_ffn_w_down))
    arrays = {
        "x": np.asarray(x),
        "conv_k": np.asarray(L0_conv_kernel).reshape(TAPS, GC, GROUPS, GC).transpose(2, 1, 0, 3).reshape(P, TAPS, GC),
        "conv_b": np.asarray(L0_conv_bias),
        "router_t": np.asarray(L0_ffn_router_w).T,
        "expert_w": np.concatenate(
            [w.reshape(E, P, J, P).transpose(1, 0, 2, 3) for w in (gate, up)]
            + [down.reshape(E, J, P, P).transpose(2, 0, 1, 3)], axis=2),
    }
    arrays = {k: np.ascontiguousarray(a) for k, a in arrays.items()}
    nc = bacc.Bacc("TRN2", target_bir_lowering=False, num_devices=1)
    args = [nc.dram_tensor(k, a.shape, mybir.dt.from_np(a.dtype), kind="ExternalInput").ap()
            for k, a in arrays.items()]
    out = nc.dram_tensor("out", arrays["x"].shape, F32, kind="ExternalOutput").ap()
    metaformer_moe(nc, *args, out)
    return run_bass_kernel_spmd(nc, [arrays], core_ids=[0]).results[0]["out"]
```

```python
from contextlib import ExitStack

import numpy as np

import concourse.bass as bass
from concourse import mybir

ALU = mybir.AluOpType
ACT = mybir.ActivationFunctionType
F32 = mybir.dt.float32
F32R = mybir.dt.float32r
U32 = mybir.dt.uint32

P = 128
IMG, HH, WW = 2, 16, 16
PAIRS = HH // 2
N = IMG * HH * WW
TT = N // P
E = 8
J = 2
GROUPS = 8
GC = P // GROUPS
CH = 2
HC = P // CH
HG = GROUPS // CH
BANDS = 2 * 3
EPS_CONV, EPS_FFN = 1e-6, 1e-5
WBQ = 4


def metaformer_moe(nc, x_rows, x_cols, conv_k, conv_b, router_t, expert_w, out_cols):
    chunks = x_rows.shape[0]
    wb_dram = nc.dram_tensor("wb_dram", [chunks, E * N], F32, kind="Internal").ap()

    with ExitStack() as ctx:
        def sb(name, shape, dt=F32):
            return ctx.enter_context(nc.sbuf_tensor(name, shape, dt))

        def sem(name):
            return ctx.enter_context(nc.semaphore(name))

        ident = sb("ident", [P, P])
        iota8 = sb("iota8", [P, E])
        neghalf = sb("neghalf", [P, TT])
        bias = sb("bias", [P, CH])
        ck = sb("ck", [P, CH * BANDS * 2, GC])
        ckc_hi, ckc_lo = sb("ckc_hi", [P, CH * BANDS * 2, GC], F32R), sb("ckc_lo", [P, CH * BANDS * 2, GC])
        own8 = sb("own8", [P, GROUPS, GC])
        own = sb("own", [P, HG, GC])
        ck_hi, ck_lo = sb("ck_hi", [P, CH * BANDS, P], F32R), sb("ck_lo", [P, CH * BANDS, P], F32R)
        rw = sb("rw", [P, E])
        rw_parts = sb("rw_parts", [P, 2 * E], F32R)
        rw_hi, rw_lo = rw_parts[:, 0:E], rw_parts[:, E:2 * E]
        ew = sb("ew", [P, E, 3 * J, P])
        ew_hi, ew_lo = sb("ew_hi", [P, E, 3 * J, P], F32R), sb("ew_lo", [P, E, 3 * J, P], F32R)
        xt = [sb(f"xt{b}", [P, TT, P]) for b in range(2)]
        xc = [sb(f"xc{b}", [P, N]) for b in range(2)]
        xn = sb("xn", [P, CH * IMG, P])
        pad_hi = sb("pad_hi", [P, CH * IMG, PAIRS + 1, WW + 2], F32R)
        pad_lo = sb("pad_lo", [P, CH * IMG, PAIRS + 1, WW + 2], F32R)
        relu = sb("relu", [P, N])
        tc = sb("tc", [P, N])
        zn = sb("zn", [P, TT, P])
        z_hi = [sb(f"z_hi{b}", [P, N], F32R) for b in range(2)]
        z_lo = [sb(f"z_lo{b}", [P, N], F32R) for b in range(2)]
        bn1, bn2 = sb("bn1", [P, TT, 6]), sb("bn2", [P, TT, 6])
        mv1, mv2 = sb("mv1", [P, TT, 2]), sb("mv2", [P, TT, 2])
        ve1, ve2 = sb("ve1", [P, TT]), sb("ve2", [P, TT])
        rstd1, rstd2 = sb("rstd1", [P, TT]), sb("rstd2", [P, TT])
        logits = sb("logits", [P, TT, E])
        top = sb("top", [P, TT, E])
        topi = sb("topi", [P, TT, E], U32)
        gap = sb("gap", [P, TT])
        th = sb("th", [P, TT])
        w12 = sb("w12", [P, 2, TT])
        hot = sb("hot", [P, 2, E, TT])
        dense = sb("dense", [P, P])
        denseT = sb("denseT", [E * TT, P])
        wb = [sb(f"wb{b}", [P, E, N]) for b in range(2)]
        sg = sb("sg", [P, 2, J, N])
        hh = sb("hh", [P, 2, J, N])
        h_hi, h_lo = sb("h_hi", [P, 2, J, N], F32R), sb("h_lo", [P, 2, J, N], F32R)
        yw = sb("yw", [P, 2, N])
        acc = [sb(f"acc{b}", [P, N]) for b in range(2)]

        ps_g = [ctx.enter_context(nc.psum_tensor(f"ps_g{j}", [P, N], F32)) for j in range(J)]
        ps_u = [ctx.enter_context(nc.psum_tensor(f"ps_u{j}", [P, N], F32)) for j in range(J)]
        ps_y = [ctx.enter_context(nc.psum_tensor(f"ps_y{b}", [P, N], F32)) for b in range(2)]
        ps_a = ctx.enter_context(nc.psum_tensor("ps_a", [P, N], F32))
        ps_b = ctx.enter_context(nc.psum_tensor("ps_b", [P, N], F32))
        conv_ps = [ps_b, ps_a]

        x_loaded = [sem(f"x_loaded{b}") for b in range(2)]
        xc_loaded = [sem(f"xc_loaded{b}") for b in range(2)]
        ck_loaded, bias_loaded, rw_loaded = sem("ck_loaded"), sem("bias_loaded"), sem("rw_loaded")
        ew_loaded = [sem(f"ew_loaded{q}") for q in range(E)]
        wb_out, out_stored = sem("wb_out"), sem("out_stored")
        wb_loaded = [sem(f"wb_loaded{q}") for q in range(WBQ)]
        ident_zeroed, ident_ready, consts_ready, own_ready = (
            sem("ident_zeroed"), sem("ident_ready"), sem("consts_ready"), sem("own_ready"))
        ckc_hi_ready, ckc_lo_ready = sem("ckc_hi_ready"), sem("ckc_lo_ready")
        neghalf_ready, iota_ready = sem("neghalf_ready"), sem("iota_ready")
        ck_hi_ready, ck_lo_ready = sem("ck_hi_ready"), sem("ck_lo_ready")
        rw_hi_ready, rw_lo_ready = sem("rw_hi_ready"), sem("rw_lo_ready")
        ew_hi_ready, ew_lo_ready = sem("ew_hi_ready"), sem("ew_lo_ready")
        mv1_ready, xn_ready, xnT_ready = sem("mv1_ready"), sem("xn_ready"), sem("xnT_ready")
        rstd1_ready, rstd2_ready = sem("rstd1_ready"), sem("rstd2_ready")
        pad_hi_ready, pad_lo_ready, conv_ready = sem("pad_hi_ready"), sem("pad_lo_ready"), sem("conv_ready")
        relu_ready, t_ready, t_rows_ready = sem("relu_ready"), sem("t_ready"), sem("t_rows_ready")
        mv2_ready, zn_ready, znT_ready = sem("mv2_ready"), sem("zn_ready"), sem("znT_ready")
        z_hi_ready, z_lo_ready, logits_ready = sem("z_hi_ready"), sem("z_lo_ready"), sem("logits_ready")
        gap_ready, th_ready, dense_ready = sem("gap_ready"), sem("th_ready"), sem("dense_ready")
        denseT_ps_ready, denseT_ready = sem("denseT_ps_ready"), sem("denseT_ready")
        passed = sem("passed")
        bn1_ready, bn2_ready = sem("bn1_ready"), sem("bn2_ready")
        ve1_ready, ve2_ready = sem("ve1_ready"), sem("ve2_ready")
        route_step = sem("route_step")
        g_ready, u_ready, sg_ready, h_ready = sem("g_ready"), sem("u_ready"), sem("sg_ready"), sem("h_ready")
        h_hi_ready, h_lo_ready, y_ready = sem("h_hi_ready"), sem("h_lo_ready"), sem("y_ready")
        yw_ready, acc_ready = sem("yw_ready"), sem("acc_ready")

        parities = [(slice(0, HC), 0), (slice(HC, P), 1)]
        banded = "p (q j w) -> p q j w"
        tile4 = "p (t c) -> p t c"

        def spread(engine, dst, src, done):
            engine.tensor_tensor(
                dst[:].rearrange("p k (a g o) -> p (k a) g o", a=2, g=HG),
                src.rearrange("p k (g o) -> p k g o", g=1).broadcast_to([P, CH * BANDS * 2, HG, GC]),
                own[:].rearrange("p (k g) o -> p k g o", k=1).broadcast_to([P, CH * BANDS * 2, HG, GC]),
                ALU.mult).then_inc(done, 1)

        block = ctx.enter_context(nc.Block())

        @block.sync
        def _(sp):
            def load_x(n, b):
                sp.dma_start(xt[b][:], x_rows[bass.ds(n, 1)].rearrange("a p t c -> p (a t) c")
                             ).then_inc(x_loaded[b], 16)
                if not isinstance(n, int) or n >= 1:
                    load_xc(n, b)

            def load_xc(n, b):
                sp.dma_start(xc[b][:], x_cols[bass.ds(n, 1)].rearrange("a p m -> (a p) m")).then_inc(xc_loaded[b], 16)

            load_x(0, 0)
            for e in range(E):
                if e == 1:
                    load_xc(0, 0)
                if e == 2:
                    load_x(1, 1)
                sp.dma_start(ew[:, e], expert_w[:, e]).then_inc(ew_loaded[e], 16)

            def routing(n, b):
                sp.wait_ge(denseT_ready, n + 1)
                sp.sem_inc(passed, 1)
                sp.dma_start(wb_dram[bass.ds(n, 1), :].rearrange("a (r p) -> (a r) p", p=P),
                             denseT[:]).then_inc(wb_out, 16)
                sp.wait_ge(wb_out, 16 * n + 16)
                sp.sem_inc(passed, 1)
                if not isinstance(n, int) or n >= 2:
                    sp.wait_ge(yw_ready, E * (n - 1))
                    sp.sem_inc(passed, 1)
                for q in range(WBQ):
                    lo, hi = q * E * N // WBQ, (q + 1) * E * N // WBQ
                    src = wb_dram[bass.ds(n, 1), lo:hi]
                    sp.dma_start(wb[b][:, q * E // WBQ:(q + 1) * E // WBQ, :].rearrange("p e n -> p (e n)"),
                                 src.broadcast_to([P, hi - lo])).then_inc(wb_loaded[q], 16)

            def store(n, b):
                sp.wait_ge(acc_ready, E * (n + 1))
                sp.sem_inc(passed, 1)
                sp.wait_ge(out_stored, 16 * (n + 1))
                sp.sem_inc(passed, 1)
                sp.dma_start(out_cols[bass.ds(n, 1)].rearrange("a p m -> (a p) m"), acc[b][:]).then_inc(out_stored, 16)

            def chunk(c, b, first=False, load=True):
                routing(c, b)
                if not first:
                    store(c - 1, 1 - b)
                if load:
                    sp.wait_ge(t_ready, c + 1)
                    sp.sem_inc(passed, 1)
                    load_x(c + 2, b)

            chunk(0, 0, first=True)
            with sp.Fori(0, (chunks - 4) // 2) as i:
                chunk(2 * i + 1, 1)
                chunk(2 * i + 2, 0)
            chunk(chunks - 3, 1)
            chunk(chunks - 2, 0, load=False)
            chunk(chunks - 1, 1, load=False)
            for half in range(2):
                cols = slice(half * N // 2, (half + 1) * N // 2)
                sp.wait_ge(acc_ready, E * chunks + half)
                sp.dma_start(out_cols[chunks - 1, :, cols], acc[1][:, cols]).then_inc(out_stored, 16)
            sp.wait_ge(out_stored, 16 * (chunks + 2))

        @block.tensor
        def _(pe):
            def transposes(dst, src, done):
                for t in range(TT):
                    last = nc.tensor.transpose(dst[:, t * P:(t + 1) * P], src(t), ident[:])
                last.then_inc(done, 1)

            def product(dst, w_hi, w_lo, v_hi, v_lo, start, stop):
                nc.tensor.matmul(dst, w_hi, v_lo, start=start, stop=False)
                nc.tensor.matmul(dst, w_hi, v_hi, start=False, stop=False)
                return nc.tensor.matmul(dst, w_lo, v_hi, start=False, stop=stop)

            def transpose_xn(n):
                pe.wait_ge(xn_ready, n + 1)
                if not isinstance(n, int) or n >= 1:
                    pe.wait_ge(gap_ready, n)
                transposes(ps_a, lambda q: xn[:, q, :], xnT_ready)

            def conv(n):
                pe.wait_ge(pad_hi_ready, 2 * n + 2)
                if not isinstance(n, int) or n >= 1:
                    pe.wait_ge(denseT_ready, n)
                for h in range(CH):
                    dst = conv_ps[h][:, 0:N // CH].rearrange(banded, q=IMG, j=PAIRS)
                    for step, (w, v) in enumerate([(ck_hi, pad_hi), (ck_lo, pad_hi), (ck_hi, pad_lo)]):
                        if isinstance(n, int) and n == 0 and h == 0 and step == 1:
                            pe.wait_ge(ck_lo_ready, 1)
                        if h == 0 and step == 2:
                            pe.wait_ge(pad_lo_ready, n + 1)
                        for k in range(BANDS):
                            below, dx = divmod(k, 3)
                            last = nc.tensor.matmul(
                                dst, w[:, h * BANDS + k, :],
                                v[:, h * IMG:(h + 1) * IMG, below:below + PAIRS, dx:dx + WW],
                                start=step == 0 and k == 0, stop=step == 2 and k == BANDS - 1)
                    last.then_inc(conv_ready, 1)

            def transpose_t(n):
                pe.wait_ge(t_ready, n + 1)
                transposes(ps_a, lambda t: tc[:, t * P:(t + 1) * P], t_rows_ready)

            def transpose_zn(n):
                pe.wait_ge(zn_ready, n + 1)
                transposes(ps_b, lambda t: zn[:, t, :], znT_ready)

            def route(n, b):
                pe.wait_ge(z_hi_ready, n + 1)
                pe.wait_ge(z_lo_ready, n + 1)
                for t in range(TT):
                    dst = ps_a[:, t * 2 * E:(t + 1) * 2 * E]
                    cols = slice(t * P, (t + 1) * P)
                    nc.tensor.matmul(dst, z_lo[b][:, cols], rw_parts[:], start=True, stop=False)
                    last = nc.tensor.matmul(dst, z_hi[b][:, cols], rw_parts[:], start=False, stop=True)
                last.then_inc(logits_ready, 1)

            def transpose_dense(n):
                pe.wait_ge(dense_ready, n + 1)
                nc.tensor.transpose(ps_b[:, 0:P], dense[:], ident[:]).then_inc(denseT_ps_ready, 1)

            def gate_up(u, e, j, b, first):
                if first:
                    pe.wait_ge(ew_hi_ready, e + 1)
                    pe.wait_ge(ew_lo_ready, e + 1)
                if not first or e >= 1:
                    pe.wait_ge(sg_ready, 2 * u - 1 + j)
                product(ps_g[j][:], ew_hi[:, e, j, :], ew_lo[:, e, j, :], z_hi[b][:], z_lo[b][:],
                        True, True).then_inc(g_ready, 1)
                if not first or e >= 1:
                    pe.wait_ge(h_ready, 2 * u - 1 + j)
                product(ps_u[j][:], ew_hi[:, e, J + j, :], ew_lo[:, e, J + j, :], z_hi[b][:], z_lo[b][:],
                        True, True).then_inc(u_ready, 1)

            def down(u, e, ub, first=False):
                if not first or e >= 2:
                    pe.wait_ge(yw_ready, u - 1)
                for j in range(J):
                    pe.wait_ge(h_hi_ready, 2 * u + j + 1)
                    pe.wait_ge(h_lo_ready, 2 * u + j + 1)
                    last = product(ps_y[ub][:], ew_hi[:, e, 2 * J + j, :], ew_lo[:, e, 2 * J + j, :],
                                   h_hi[:, ub, j, :], h_lo[:, ub, j, :], j == 0, j == J - 1)
                last.then_inc(y_ready, 1)

            def chunk(c, b, first=False, last=False, ahead=True):
                n, m = c + 1, c + 2
                for e in range(E):
                    u = c * E + e
                    gate_up(u, e, 0, b, first)
                    if e == 0 and not first:
                        transpose_dense(c)
                    gate_up(u, e, 1, b, first)
                    if e == 1 and first:
                        transpose_xn(n)
                    if e == 2 and not last:
                        conv(n)
                    if e == 3 and not last:
                        transpose_t(n)
                    if e == 5 and not last:
                        transpose_zn(n)
                    if e == 6 and not last:
                        route(n, 1 - b)
                    if not first or e >= 1:
                        down(u - 1, (e - 1) % E, (e - 1) % 2, first)
                    if e == 0 and first:
                        transpose_dense(c)
                    if e == 7 and ahead:
                        transpose_xn(m)

            def keep_warm(times):
                for _ in range(times):
                    nc.tensor.matmul(ps_y[0][:, 0:P], ident[:], ident[:], start=True, stop=True)

            pe.wait_ge(ident_ready, 1)
            keep_warm(12)
            transpose_xn(0)
            keep_warm(4)
            pe.wait_ge(ck_hi_ready, 1)
            conv(0)
            transpose_t(0)
            keep_warm(16)
            transpose_zn(0)
            keep_warm(4)
            pe.wait_ge(rw_hi_ready, 1)
            pe.wait_ge(rw_lo_ready, 1)
            route(0, 0)
            chunk(0, 0, first=True)
            with pe.Fori(0, (chunks - 4) // 2) as i:
                chunk(2 * i + 1, 1)
                chunk(2 * i + 2, 0)
            chunk(chunks - 3, 1)
            chunk(chunks - 2, 0, ahead=False)
            chunk(chunks - 1, 1, last=True, ahead=False)
            down(chunks * E - 1, E - 1, 1)

        @block.scalar
        def _(act):
            def pad_heads(n):
                act.wait_ge(xnT_ready, n + 1)
                for rows, par in parities:
                    last = nc.scalar.copy(pad_hi[rows, :, par:par + PAIRS, 1:1 + WW],
                                          ps_a[rows, :].rearrange(banded, q=CH * IMG, j=PAIRS))
                    last.then_inc(pad_hi_ready, 1)

            def conv_relu(n):
                if not isinstance(n, int) or n >= 1:
                    act.wait_ge(t_ready, n)
                for h in range(CH):
                    act.wait_ge(conv_ready, CH * n + h + 1)
                    for rows, par in parities:
                        last = nc.scalar.activation(
                            relu[h * HC:(h + 1) * HC, :].rearrange("p (b k m) -> p b k m", b=IMG, k=2)[:, :, par, :],
                            conv_ps[h][rows, 0:N // CH].rearrange("p (b m) -> p b m", b=IMG),
                            ACT.Relu, bias=bias[rows, h:h + 1])
                last.then_inc(relu_ready, 1)

            def z_heads(n, b):
                act.wait_ge(znT_ready, n + 1)
                nc.scalar.copy(z_hi[b][:], ps_b[:]).then_inc(z_hi_ready, 1)

            def pair_weight(n):
                act.wait_ge(gap_ready, n + 1)
                nc.scalar.activation(th[:], gap[:], ACT.Tanh, scale=0.5).then_inc(th_ready, 1)

            def dense_rows(n):
                act.wait_ge(denseT_ps_ready, n + 1)
                if not isinstance(n, int) or n >= 1:
                    act.wait_ge(wb_out, 16 * n)
                nc.scalar.copy(denseT[:], ps_b[0:E * TT, 0:P]).then_inc(denseT_ready, 1)

            def chunk(c, b, first=False, last=False):
                n = c + 1
                for e in range(E):
                    u, ub = c * E + e, e % 2
                    for j in range(J):
                        act.wait_ge(g_ready, 2 * u + j + 1)
                        if not first or e >= 2:
                            act.wait_ge(h_ready, 2 * u - 3 + j)
                        nc.scalar.activation(sg[:, ub, j, :], ps_g[j][:], ACT.Silu).then_inc(sg_ready, 1)
                        if e == 0 and j == 0:
                            dense_rows(c)
                        if e == (1 if first else 0) and j == 1 and not last:
                            pad_heads(n)
                        if e == 5 and j == 0 and not last:
                            z_heads(n, 1 - b)
                    for j in range(J):
                        act.wait_ge(h_ready, 2 * u + j + 1)
                        if not first or e >= 2:
                            act.wait_ge(y_ready, u - 1)
                        nc.scalar.copy(h_hi[:, ub, j, :], hh[:, ub, j, :]).then_inc(h_hi_ready, 1)
                    if e == 2 and not last:
                        conv_relu(n)
                    if e == 6 and not last:
                        pair_weight(n)

            act.dma_start(ck[:], conv_k).then_inc(ck_loaded, 16)
            act.dma_start(bias[:], conv_b).then_inc(bias_loaded, 16)
            act.dma_start(rw[:], router_t).then_inc(rw_loaded, 16)
            act.wait_ge(neghalf_ready, 1)
            nc.scalar.activation(th[:], neghalf[:], ACT.Silu)
            act.wait_ge(consts_ready, 3)
            pad_heads(0)
            act.wait_ge(rw_loaded, 16)
            nc.scalar.copy(rw_hi, rw[:]).then_inc(rw_hi_ready, 1)

            def weight_heads(e):
                act.wait_ge(ew_loaded[e], 16)
                nc.scalar.copy(ew_hi[:, e], ew[:, e]).then_inc(ew_hi_ready, 1)

            for e in (0, 1, 2, 3):
                weight_heads(e)
            act.wait_ge(bias_loaded, 16)
            conv_relu(0)
            weight_heads(4)
            weight_heads(5)
            z_heads(0, 0)
            weight_heads(6)
            weight_heads(7)
            pair_weight(0)
            chunk(0, 0, first=True)
            with act.Fori(0, (chunks - 4) // 2) as i:
                chunk(2 * i + 1, 1)
                chunk(2 * i + 2, 0)
            chunk(chunks - 3, 1)
            chunk(chunks - 2, 0)
            chunk(chunks - 1, 1, last=True)

        @block.vector
        def _(dve):
            def ln_stats(src, bn, mv, before, bn_ready, done):
                for t in range(TT):
                    nc.vector.bn_stats(bn[:, t, :], src(t)).then_inc(bn_ready, 1)
                dve.wait_ge(bn_ready, before + TT)
                dve.sem_inc(passed, 1)
                for t in range(TT):
                    last = nc.vector.bn_aggr(mv[:, t, :], bn[:, t, :])
                last.then_inc(done, 1)

            def ln_apply(src, mv, rstd, dst, done):
                for t in range(TT):
                    last = nc.vector.tensor_scalar(dst(t), src(t), mv[:, t, 0:1], rstd[:, t:t + 1],
                                                   ALU.subtract, ALU.mult)
                last.then_inc(done, 1)

            def normalise_x(n, b):
                dve.wait_ge(rstd1_ready, n + 1)
                if not isinstance(n, int) or n >= 1:
                    dve.wait_ge(xnT_ready, n)
                ln_apply(lambda t: xt[b][:, t, :].rearrange("p (h c) -> p h c", h=CH), mv1, rstd1,
                         lambda t: xn[:].rearrange("p (h b) (k c) -> p h b k c", h=CH, k=2)[:, :, t // 2, t % 2, :],
                         xn_ready)

            def normalise_t(n):
                dve.wait_ge(rstd2_ready, n + 1)
                if not isinstance(n, int) or n >= 1:
                    dve.wait_ge(znT_ready, n)
                ln_apply(lambda t: ps_a[:, t * P:(t + 1) * P], mv2, rstd2, lambda t: zn[:, t, :], zn_ready)

            STEPS = TT + 5

            def stats_x(n, b):
                dve.wait_ge(x_loaded[b], 8 * n + 16 - 8 * b)
                ln_stats(lambda t: xt[b][:, t, :], bn1, mv1, n * TT, bn1_ready, mv1_ready)

            def pad_tails(n):
                for rows, par in parities:
                    dve.wait_ge(pad_hi_ready, 2 * n + par + 1)
                    part = (rows, slice(None), slice(par, par + PAIRS), slice(1, 1 + WW))
                    last = nc.vector.tensor_tensor(pad_lo[part], ps_a[rows, :].rearrange(banded, q=CH * IMG, j=PAIRS),
                                                   pad_hi[part].bitcast(F32), ALU.subtract)
                last.then_inc(pad_lo_ready, 1)

            def residual(n, b):
                dve.wait_ge(relu_ready, n + 1)
                dve.wait_ge(xc_loaded[b], 8 * n + 16 - 8 * b)
                if not isinstance(n, int) or n >= 1:
                    dve.wait_ge(acc_ready, E * (n - 1) + 1)
                nc.vector.tensor_tensor(tc[:], relu[:], xc[b][:], ALU.add).then_inc(t_ready, 1)

            def stats_t(n):
                dve.wait_ge(t_rows_ready, n + 1)
                ln_stats(lambda t: ps_a[:, t * P:(t + 1) * P], bn2, mv2, n * TT, bn2_ready, mv2_ready)

            def z_tails(n, b):
                dve.wait_ge(z_hi_ready, n + 1)
                nc.vector.tensor_tensor(z_lo[b][:], ps_b[:], z_hi[b][:].bitcast(F32), ALU.subtract
                                        ).then_inc(z_lo_ready, 1)

            def top_two(n):
                s = n * STEPS
                dve.wait_ge(logits_ready, n + 1)
                nc.vector.tensor_reduce(logits[:], ps_a[:, 0:TT * 2 * E].rearrange("p (t k e) -> p t e k", t=TT, k=2),
                                        mybir.AxisListType.X, ALU.add).then_inc(route_step, 1)
                dve.wait_ge(route_step, s + 1)
                dve.sem_inc(passed, 1)
                for t in range(TT):
                    nc.vector.max(top[:, t, :], logits[:, t, :]).then_inc(route_step, 1)
                dve.wait_ge(route_step, s + 1 + TT)
                nc.vector.tensor_tensor(gap[:], top[:, :, 0], top[:, :, 1], ALU.subtract).then_inc(gap_ready, 1)
                for t in range(TT):
                    last = nc.vector.max_index(topi[:, t, :], top[:, t, :], logits[:, t, :])
                last.then_inc(route_step, 1)
                dve.wait_ge(route_step, s + 2 + TT)
                for k in range(2):
                    last = nc.vector.tensor_tensor(
                        hot[:, k], topi[:, :, k:k + 1].rearrange("p t o -> p o t").broadcast_to([P, E, TT]),
                        iota8[:].rearrange("p (e o) -> p e o", o=1).broadcast_to([P, E, TT]), ALU.is_equal)
                last.then_inc(route_step, 1)

            def dense_weights(n):
                s = n * STEPS + TT
                dve.wait_ge(th_ready, n + 1)
                nc.vector.tensor_scalar(w12[:, 0, :], th[:], 0.5, 0.5, ALU.mult, ALU.add)
                nc.vector.tensor_scalar(w12[:, 1, :], th[:], -0.5, 0.5, ALU.mult, ALU.add).then_inc(route_step, 1)
                dve.wait_ge(route_step, s + 4)
                for k in range(2):
                    last = nc.vector.tensor_tensor(hot[:, k], hot[:, k],
                                                   w12[:, k:k + 1, :].broadcast_to([P, E, TT]), ALU.mult)
                last.then_inc(route_step, 1)
                dve.wait_ge(route_step, s + 5)
                nc.vector.tensor_tensor(dense[:, 0:E * TT], hot[:, 0].rearrange("p e t -> p (e t)"),
                                        hot[:, 1].rearrange("p e t -> p (e t)"), ALU.add).then_inc(dense_ready, 1)

            def weigh(c, b, e, first=False):
                u, ub = c * E + e, e % 2
                if e % (E // WBQ) == 0:
                    dve.wait_ge(wb_loaded[e * WBQ // E], 16 * c + 16)
                dve.wait_ge(y_ready, u + 1)
                if not first or e >= 2:
                    dve.wait_ge(acc_ready, u - 1)
                nc.vector.tensor_tensor(yw[:, ub, :], ps_y[ub][:], wb[b][:, e, :], ALU.mult).then_inc(yw_ready, 1)

            def chunk(c, b, first=False, last=False, ahead=True):
                n, m = c + 1, c + 2
                for e in range(E):
                    u, ub = c * E + e, e % 2
                    if e == 3 and not last:
                        residual(n, 1 - b)
                    for j in range(J):
                        if e == 2 and j == 1:
                            weigh(c, b, 0, first)
                        dve.wait_ge(sg_ready, 2 * u + j + 1)
                        dve.wait_ge(u_ready, 2 * u + j + 1)
                        nc.vector.tensor_tensor(hh[:, ub, j, :], ps_u[j][:], sg[:, ub, j, :], ALU.mult
                                                ).then_inc(h_ready, 1)
                    if e == 4 and not last:
                        normalise_t(n)
                    if e == 5 and not last:
                        z_tails(n, 1 - b)
                    if e == 7 and not last:
                        dense_weights(n)
                    if e == 0 and first:
                        normalise_x(n, 1 - b)
                    for j in range(J):
                        dve.wait_ge(h_hi_ready, 2 * u + j + 1)
                        nc.vector.tensor_tensor(h_lo[:, ub, j, :], hh[:, ub, j, :],
                                                h_hi[:, ub, j, :].bitcast(F32), ALU.subtract).then_inc(h_lo_ready, 1)
                    if e == (1 if first else 0) and not last:
                        pad_tails(n)
                    if e == 3 and not last:
                        stats_t(n)
                    if e == 6 and not last:
                        top_two(n)
                    if e == 2 and ahead:
                        stats_x(m, b)
                    if e >= 2:
                        weigh(c, b, e - 1, first)
                    elif e == 0 and not first:
                        weigh(c - 1, 1 - b, E - 1)
                    if e == 3 and ahead:
                        normalise_x(m, b)

            stats_x(0, 0)
            dve.wait_ge(ck_loaded, 16)
            nc.vector.tensor_copy(ckc_hi[:], ck[:]).then_inc(ckc_hi_ready, 1)
            dve.wait_ge(ckc_hi_ready, 1)
            nc.vector.tensor_tensor(ckc_lo[:], ck[:], ckc_hi[:].bitcast(F32), ALU.subtract).then_inc(ckc_lo_ready, 1)
            normalise_x(0, 0)
            dve.wait_ge(own_ready, 4)
            spread(nc.vector, ck_hi, ckc_hi[:].bitcast(F32), ck_hi_ready)
            dve.wait_ge(consts_ready, 3)
            pad_tails(0)
            dve.wait_ge(rw_hi_ready, 1)
            nc.vector.tensor_tensor(rw_lo, rw[:], rw_hi.bitcast(F32), ALU.subtract).then_inc(rw_lo_ready, 1)

            residual(0, 0)
            stats_t(0)
            normalise_t(0)
            z_tails(0, 0)
            stats_x(1, 1)
            dve.wait_ge(iota_ready, 1)
            top_two(0)
            dense_weights(0)
            chunk(0, 0, first=True)
            with dve.Fori(0, (chunks - 4) // 2) as i:
                chunk(2 * i + 1, 1)
                chunk(2 * i + 2, 0)
            chunk(chunks - 3, 1)
            chunk(chunks - 2, 0, ahead=False)
            chunk(chunks - 1, 1, last=True, ahead=False)
            weigh(chunks - 1, 1, E - 1)
            dve.wait_ge(yw_ready, chunks * E)
            dve.wait_ge(acc_ready, chunks * E - 1)
            for half in range(2):
                cols = slice(half * N // 2, (half + 1) * N // 2)
                nc.vector.tensor_tensor(acc[1][:, cols], acc[1][:, cols], yw[:, (E - 1) % 2, cols], ALU.add
                                        ).then_inc(acc_ready, 1)

        @block.gpsimd
        def _(pool):
            def inverse_std(n, mv, eps, ve, ve_ready, rstd, done):
                pool.sem_inc(passed, 1)
                nc.gpsimd.tensor_scalar(ve[:], mv[:, :, 1], 1.0, eps, ALU.mult, ALU.add).then_inc(ve_ready, 1)
                pool.wait_ge(ve_ready, n + 1)
                nc.gpsimd.tensor_tensor(rstd[:], ve[:], neghalf[:], ALU.pow).then_inc(done, 1)

            def rstd_x(n):
                pool.wait_ge(mv1_ready, n + 1)
                inverse_std(n, mv1, EPS_CONV, ve1, ve1_ready, rstd1, rstd1_ready)

            def rstd_t(n):
                pool.wait_ge(mv2_ready, n + 1)
                inverse_std(n, mv2, EPS_FFN, ve2, ve2_ready, rstd2, rstd2_ready)

            def accumulate(c, b, e):
                u = c * E + e
                pool.wait_ge(yw_ready, u + 1)
                if e == 0:
                    if not isinstance(c, int) or c >= 1:
                        pool.wait_ge(out_stored, 16 * c)
                else:
                    pool.wait_ge(acc_ready, u)
                nc.gpsimd.tensor_tensor(acc[b][:], tc[:] if e == 0 else acc[b][:], yw[:, e % 2, :], ALU.add
                                        ).then_inc(acc_ready, 1)

            def chunk(c, b, first=False, last=False, ahead=True):
                n, m = c + 1, c + 2
                for e in range(E):
                    if e == 3 and ahead:
                        rstd_x(m)
                    if e == 3 and not last:
                        rstd_t(n)
                    if e >= 1:
                        accumulate(c, b, e - 1)
                    if e == 0 and not first:
                        accumulate(c - 1, 1 - b, E - 1)

            def weight_tails(e):
                pool.wait_ge(ew_hi_ready, e + 1)
                nc.gpsimd.tensor_tensor(ew_lo[:, e], ew[:, e], ew_hi[:, e].bitcast(F32), ALU.subtract
                                        ).then_inc(ew_lo_ready, 1)

            nc.gpsimd.memset(ident[:], 0.0).then_inc(ident_zeroed, 1)
            nc.gpsimd.memset(neghalf[:], -0.5).then_inc(neghalf_ready, 1)
            pool.wait_ge(ident_zeroed, 1)
            nc.gpsimd.affine_select(out=ident[:], in_=ident[:], compare_op=ALU.not_equal, fill=1.0, base=0,
                                    pattern=[[-1, P]], channel_multiplier=1).then_inc(ident_ready, 1)
            nc.gpsimd.memset(own8[:], 1.0).then_inc(own_ready, 1)
            pool.wait_ge(own_ready, 1)
            nc.gpsimd.affine_select(out=own8[:], in_=own8[:], compare_op=ALU.is_ge, fill=0.0, base=0,
                                    pattern=[[-GC, GROUPS], [0, GC]], channel_multiplier=1).then_inc(own_ready, 1)
            pool.wait_ge(own_ready, 2)
            nc.gpsimd.affine_select(out=own8[:], in_=own8[:], compare_op=ALU.is_ge, fill=0.0, base=GC - 1,
                                    pattern=[[GC, GROUPS], [0, GC]], channel_multiplier=-1).then_inc(own_ready, 1)
            pool.wait_ge(own_ready, 3)
            nc.gpsimd.tensor_tensor(own[:], own8[:, 0:HG], own8[:, HG:GROUPS], ALU.add).then_inc(own_ready, 1)
            nc.gpsimd.memset(pad_hi[:].bitcast(F32), 0.0).then_inc(consts_ready, 1)
            nc.gpsimd.memset(pad_lo[:].bitcast(F32), 0.0).then_inc(consts_ready, 1)
            nc.gpsimd.memset(dense[:], 0.0).then_inc(consts_ready, 1)
            nc.gpsimd.iota(iota8[:], pattern=[[1, E]], base=0, channel_multiplier=0,
                           allow_small_or_imprecise_dtypes=True).then_inc(iota_ready, 1)
            pool.wait_ge(neghalf_ready, 1)
            rstd_x(0)
            pool.wait_ge(ckc_lo_ready, 1)
            spread(nc.gpsimd, ck_lo, ckc_lo[:], ck_lo_ready)
            for e in (0, 1, 2):
                weight_tails(e)
            rstd_t(0)
            for e in range(3, E):
                weight_tails(e)
                if e == 4:
                    rstd_x(1)
            pool.sem_inc(out_stored, 16)
            chunk(0, 0, first=True)
            with pool.Fori(0, (chunks - 4) // 2) as i:
                chunk(2 * i + 1, 1)
                chunk(2 * i + 2, 0)
            chunk(chunks - 3, 1)
            chunk(chunks - 2, 0, ahead=False)
            chunk(chunks - 1, 1, last=True, ahead=False)


def kernel(x, L0_conv_kernel, L0_conv_bias, L0_ffn_router_w, L0_ffn_w_gate, L0_ffn_w_up, L0_ffn_w_down):
    import concourse.bacc as bacc
    from concourse.bass_utils import run_bass_kernel_spmd

    gate, up, down = (np.asarray(w) for w in (L0_ffn_w_gate, L0_ffn_w_up, L0_ffn_w_down))
    x = np.asarray(x)
    chunks = x.shape[0] // IMG
    tokens = x.reshape(chunks, IMG, PAIRS, 2, WW, P).transpose(0, 1, 3, 2, 4, 5).reshape(chunks, TT, P, P)
    taps = np.pad(np.asarray(L0_conv_kernel).reshape(3, 3, GC, CH, HG, GC), [(1, 1)] + [(0, 0)] * 5)
    bands = np.stack([np.stack([np.stack([taps[2 * below + 2 - odd_in - odd_out] for odd_out in range(2)])
                                for below in range(2)]) for odd_in in range(2)])
    arrays = {
        "x_rows": tokens.transpose(0, 2, 1, 3),
        "x_cols": tokens.reshape(chunks, N, P).transpose(0, 2, 1),
        "conv_k": bands.transpose(0, 6, 4, 5, 1, 3, 2, 7).reshape(P, CH * BANDS * 2, GC),
        "conv_b": np.tile(np.asarray(L0_conv_bias).reshape(CH, HC).T, (2, 1)),
        "router_t": np.asarray(L0_ffn_router_w).T,
        "expert_w": np.concatenate(
            [w.reshape(E, P, J, P).transpose(1, 0, 2, 3) for w in (gate, up)]
            + [down.reshape(E, J, P, P).transpose(2, 0, 1, 3)], axis=2),
    }
    arrays = {k: np.ascontiguousarray(a) for k, a in arrays.items()}
    nc = bacc.Bacc("TRN2", target_bir_lowering=False, num_devices=1)
    args = [nc.dram_tensor(k, a.shape, mybir.dt.from_np(a.dtype), kind="ExternalInput").ap()
            for k, a in arrays.items()]
    out = nc.dram_tensor("out", [chunks, P, N], F32, kind="ExternalOutput").ap()
    metaformer_moe(nc, *args, out)
    cols = run_bass_kernel_spmd(nc, [arrays], core_ids=[0]).results[0]["out"]
    return cols.reshape(chunks, P, IMG, 2, PAIRS, WW).transpose(0, 2, 4, 3, 5, 1).reshape(x.shape)
```
